# Optimizing a Trainium2 kernel written in Bass

```python
import numpy as np
import jax
import jax.numpy as jnp

def _softmax(x, axis=-1):
    return jax.nn.softmax(x, axis=axis)

def _gelu(x):
    return jax.nn.gelu(x, approximate=True)

def _silu(x):
    return jax.nn.silu(x)

def _sigmoid(x):
    return jax.nn.sigmoid(x)

def _layernorm(x, axis=-1, eps=1e-05):
    m = jnp.mean(x, axis=axis, keepdims=True)
    v = jnp.var(x, axis=axis, keepdims=True)
    return (x - m) / jnp.sqrt(v + eps)

def _scatter_add(tgt, idx, src, axis=0):
    return tgt.at[idx].add(src)

def _segment_sum(src, seg, n):
    return jax.ops.segment_sum(src, seg, n)
kernel_name = 'mk_vit_tower_postln_d1_tok_img1024_r4_8a078d'

def setup_inputs(seed: int=0):
    np.random.seed(seed)
    _w = jnp.asarray

    def _rec_inputs():
        import jax
        import jax.numpy as jnp
        _rk = jax.random.key(seed)
        x = -0.000348323 + 0.999952 * jax.random.normal(jax.random.fold_in(_rk, 1), (16, 3, 96, 96), jnp.float32)
        return x
    x = _rec_inputs()

    def _L0_tok_setup():
        import jax, jax.numpy as jnp
        import numpy as np
        from jax import lax
        PATCH = 16
        key = jax.random.key(seed)
        k1, k2 = jax.random.split(key)
        B, C, IMG, HID = (32, 3, 96, 256)
        inputs = jax.random.normal(k1, (B, C, IMG, IMG), dtype=jnp.float32)
        flat = C * PATCH * PATCH
        W = jax.random.normal(k2, (flat, HID), dtype=jnp.float32) / np.sqrt(flat)
        return {'inputs': inputs, 'W': W}
    _L0_tok_all = _L0_tok_setup()
    _L0_tok_in = {k: v for k, v in _L0_tok_all.items() if k in ('W',)}
    del _L0_tok_all

    def _L0_attn_setup():
        import jax, jax.numpy as jnp
        import numpy as np
        import math
        D_MODEL = 256
        NUM_HEADS = 16
        HEAD_DIM = D_MODEL // NUM_HEADS
        LN_EPS = 1e-05

        def _layer_norm(x, g, b):
            mu = jnp.mean(x, axis=-1, keepdims=True)
            var = jnp.mean(jnp.square(x - mu), axis=-1, keepdims=True)
            return (x - mu) * jax.lax.rsqrt(var + LN_EPS) * g + b

        def _rope_tables(seq_len, dim, dtype):
            inv_freq = 1.0 / 10000.0 ** (jnp.arange(0, dim, 2, dtype=jnp.float32) / dim)
            t = jnp.arange(seq_len, dtype=jnp.float32)
            freqs = t[:, None] * inv_freq[None, :]
            emb = jnp.concatenate([freqs, freqs], axis=-1)
            return (jnp.cos(emb).astype(dtype), jnp.sin(emb).astype(dtype))

        def _rotate_half(x):
            x1, x2 = jnp.split(x, 2, axis=-1)
            return jnp.concatenate([-x2, x1], axis=-1)
        key = jax.random.key(seed)
        ks = jax.random.split(key, 8)
        B, S, D = (2, 512, D_MODEL)
        s_in = 1.0 / math.sqrt(D)
        return {'x': jax.random.normal(ks[0], (B, S, D), jnp.float32), 'ln1_g': jnp.ones((D,), jnp.float32), 'ln1_b': jnp.zeros((D,), jnp.float32), 'Wqkv': jax.random.normal(ks[1], (D, 3 * D), jnp.float32) * s_in, 'bqkv': jnp.zeros((3 * D,), jnp.float32), 'Wo': jax.random.normal(ks[2], (D, D), jnp.float32) * s_in, 'bo': jnp.zeros((D,), jnp.float32), 'ln2_g': jnp.ones((D,), jnp.float32), 'ln2_b': jnp.zeros((D,), jnp.float32), 'W1': jax.random.normal(ks[3], (D, 4 * D), jnp.float32) * s_in, 'b1': jnp.zeros((4 * D,), jnp.float32), 'W2': jax.random.normal(ks[4], (4 * D, D), jnp.float32) / math.sqrt(4 * D), 'b2': jnp.zeros((D,), jnp.float32)}
    _L0_attn_all = _L0_attn_setup()
    _L0_attn_in = {k: v for k, v in _L0_attn_all.items() if k in ('ln1_g', 'ln1_b', 'Wqkv', 'bqkv', 'Wo', 'bo', 'ln2_g', 'ln2_b', 'W1', 'b1', 'W2', 'b2')}
    del _L0_attn_all

    def _L0_ffn_setup():
        import jax, jax.numpy as jnp
        import numpy as np
        B, S, D, F, E = (4, 512, 256, 1024, 8)
        key = jax.random.key(seed)
        ks = jax.random.split(key, 7)
        s1 = 1.0 / np.sqrt(D)
        s2 = 1.0 / np.sqrt(F)
        x = jax.random.normal(ks[0], (B, S, D), dtype=jnp.float32)
        W1 = jax.random.uniform(ks[1], (E, D, F), jnp.float32, -s1, s1)
        b1 = jax.random.uniform(ks[2], (E, F), jnp.float32, -s1, s1)
        W2 = jax.random.uniform(ks[3], (E, F, D), jnp.float32, -s2, s2)
        b2 = jax.random.uniform(ks[4], (E, D), jnp.float32, -s2, s2)
        Wr = jax.random.uniform(ks[5], (D, E), jnp.float32, -s1, s1)
        br = jax.random.uniform(ks[6], (E,), jnp.float32, -s1, s1)
        return {'x': x, 'W1': W1, 'b1': b1, 'W2': W2, 'b2': b2, 'Wr': Wr, 'br': br}
    _L0_ffn_all = _L0_ffn_setup()
    _L0_ffn_in = {k: v for k, v in _L0_ffn_all.items() if k in ('W1', 'b1', 'W2', 'b2', 'Wr', 'br')}
    del _L0_ffn_all
    return {'x': x, 'L0_tok_W': _L0_tok_in['W'], 'L0_attn_ln1_g': _L0_attn_in['ln1_g'], 'L0_attn_ln1_b': _L0_attn_in['ln1_b'], 'L0_attn_Wqkv': _L0_attn_in['Wqkv'], 'L0_attn_bqkv': _L0_attn_in['bqkv'], 'L0_attn_Wo': _L0_attn_in['Wo'], 'L0_attn_bo': _L0_attn_in['bo'], 'L0_attn_ln2_g': _L0_attn_in['ln2_g'], 'L0_attn_ln2_b': _L0_attn_in['ln2_b'], 'L0_attn_W1': _L0_attn_in['W1'], 'L0_attn_b1': _L0_attn_in['b1'], 'L0_attn_W2': _L0_attn_in['W2'], 'L0_attn_b2': _L0_attn_in['b2'], 'L0_ffn_W1': _L0_ffn_in['W1'], 'L0_ffn_b1': _L0_ffn_in['b1'], 'L0_ffn_W2': _L0_ffn_in['W2'], 'L0_ffn_b2': _L0_ffn_in['b2'], 'L0_ffn_Wr': _L0_ffn_in['Wr'], 'L0_ffn_br': _L0_ffn_in['br']}

def reference(x, L0_tok_W, L0_attn_ln1_g, L0_attn_ln1_b, L0_attn_Wqkv, L0_attn_bqkv, L0_attn_Wo, L0_attn_bo, L0_attn_ln2_g, L0_attn_ln2_b, L0_attn_W1, L0_attn_b1, L0_attn_W2, L0_attn_b2, L0_ffn_W1, L0_ffn_b1, L0_ffn_W2, L0_ffn_b2, L0_ffn_Wr, L0_ffn_br):
    import jax
    import jax.numpy as jnp

    def _L0_tok_ref(inputs, W):
        import jax, jax.numpy as jnp
        import numpy as np
        from jax import lax
        PATCH = 16
        B, C, H, Wimg = inputs.shape
        patches = lax.conv_general_dilated_patches(inputs, filter_shape=[PATCH, PATCH], window_strides=[PATCH, PATCH], padding='VALID', dimension_numbers=('NCHW', 'HWIO', 'NCHW'))
        patches = patches.reshape(B, -1, C * PATCH * PATCH)
        return jnp.einsum('bnf,fh->bnh', patches, W)

    def _L0_attn_ref(x, ln1_g, ln1_b, Wqkv, bqkv, Wo, bo, ln2_g, ln2_b, W1, b1, W2, b2):
        import jax, jax.numpy as jnp
        import numpy as np
        import math
        D_MODEL = 256
        NUM_HEADS = 16
        HEAD_DIM = D_MODEL // NUM_HEADS
        LN_EPS = 1e-05

        def _layer_norm(x, g, b):
            mu = jnp.mean(x, axis=-1, keepdims=True)
            var = jnp.mean(jnp.square(x - mu), axis=-1, keepdims=True)
            return (x - mu) * jax.lax.rsqrt(var + LN_EPS) * g + b

        def _rope_tables(seq_len, dim, dtype):
            inv_freq = 1.0 / 10000.0 ** (jnp.arange(0, dim, 2, dtype=jnp.float32) / dim)
            t = jnp.arange(seq_len, dtype=jnp.float32)
            freqs = t[:, None] * inv_freq[None, :]
            emb = jnp.concatenate([freqs, freqs], axis=-1)
            return (jnp.cos(emb).astype(dtype), jnp.sin(emb).astype(dtype))

        def _rotate_half(x):
            x1, x2 = jnp.split(x, 2, axis=-1)
            return jnp.concatenate([-x2, x1], axis=-1)
        B, S, D = x.shape
        H, hd = (NUM_HEADS, HEAD_DIM)
        normed = _layer_norm(x, ln1_g, ln1_b)
        qkv = (normed @ Wqkv + bqkv).reshape(B, S, 3, H, hd)
        qkv = jnp.transpose(qkv, (2, 0, 3, 1, 4))
        q, k, v = (qkv[0], qkv[1], qkv[2])
        cos, sin = _rope_tables(S, hd, q.dtype)
        cos = cos[None, None, :, :]
        sin = sin[None, None, :, :]
        q = q * cos + _rotate_half(q) * sin
        k = k * cos + _rotate_half(k) * sin
        scores = jnp.einsum('bhqd,bhkd->bhqk', q, k) / math.sqrt(hd)
        causal = jnp.triu(jnp.ones((S, S), dtype=bool), k=1)
        scores = jnp.where(causal[None, None], -jnp.inf, scores)
        attn = jax.nn.softmax(scores, axis=-1)
        attn_out = jnp.einsum('bhqk,bhkd->bhqd', attn, v)
        attn_out = jnp.transpose(attn_out, (0, 2, 1, 3)).reshape(B, S, D)
        attn_out = attn_out @ Wo + bo
        x = x + attn_out
        h = _layer_norm(x, ln2_g, ln2_b)
        h = jax.nn.gelu(h @ W1 + b1, approximate=False) @ W2 + b2
        return x + h

    def _L0_ffn_ref(x, W1, b1, W2, b2, Wr, br):
        import jax, jax.numpy as jnp
        import numpy as np
        B, S, D, F, E = (4, 512, 256, 1024, 8)
        b, s, d = x.shape
        e = Wr.shape[1]
        logits = x @ Wr + br
        idx = jnp.argmax(logits, axis=-1)
        probs = jax.nn.softmax(logits, axis=-1)
        gates = jnp.take_along_axis(probs, idx[..., None], axis=-1)[..., 0]
        xf = x.reshape(-1, d)
        idxf = idx.reshape(-1)
        gf = gates.reshape(-1)
        out = jnp.zeros_like(xf)
        for ei in range(e):
            h = jax.nn.gelu(xf @ W1[ei] + b1[ei], approximate=False)
            y = h @ W2[ei] + b2[ei]
            mask = (idxf == ei).astype(xf.dtype)
            out = out + y * (gf * mask)[:, None]
        return out.reshape(b, s, d)
    h = _L0_tok_ref(x, L0_tok_W)
    h = _layernorm(h + _L0_attn_ref(h, L0_attn_ln1_g, L0_attn_ln1_b, L0_attn_Wqkv, L0_attn_bqkv, L0_attn_Wo, L0_attn_bo, L0_attn_ln2_g, L0_attn_ln2_b, L0_attn_W1, L0_attn_b1, L0_attn_W2, L0_attn_b2), axis=-1)
    h = _layernorm(h + _L0_ffn_ref(h, L0_ffn_W1, L0_ffn_b1, L0_ffn_W2, L0_ffn_b2, L0_ffn_Wr, L0_ffn_br), axis=-1)
    return h

_drawn_inputs = setup_inputs


def setup_inputs(seed=0):
    import zlib

    import numpy as np

    out = dict(_drawn_inputs(seed))
    spreads = {'L0_attn_ln1_g': (1.0, 0.2),
     'L0_attn_ln1_b': (0.0, 0.1),
     'L0_attn_bqkv': (0.0, 0.1),
     'L0_attn_bo': (0.0, 0.1),
     'L0_attn_ln2_g': (1.0, 0.2),
     'L0_attn_ln2_b': (0.0, 0.1),
     'L0_attn_b1': (0.0, 0.1),
     'L0_attn_b2': (0.0, 0.1)}
    factors = {'L0_ffn_b1': 8.0, 'L0_ffn_b2': 8.0, 'L0_ffn_br': 4.605}
    for name, (base, spread) in spreads.items():
        noise = np.random.default_rng([zlib.crc32(name.encode()), seed]).standard_normal(out[name].shape)
        drawn = base * np.exp(spread * noise) if base else spread * noise
        out[name] = jnp.asarray(drawn.astype(out[name].dtype))
    for name, factor in factors.items():
        out[name] = (out[name] * factor).astype(out[name].dtype)
    return out
```

```python
from contextlib import ExitStack

import numpy as np
import concourse.bass as bass
from concourse.bass import ds
from concourse import mybir

ALU = mybir.AluOpType
ACT = mybir.ActivationFunctionType
F32 = mybir.dt.float32
BF16 = mybir.dt.bfloat16
I32 = mybir.dt.int32
AX = mybir.AxisListType.X

P = 128
IMGS, SEQ, D, H, HD = 16, 36, 256, 16, 16
TOK = IMGS * SEQ
KT = D // P
TILES = [(t, min(P, TOK - t)) for t in range(0, TOK, P)]
NT = len(TILES)
PATCH_K = 3 * 16 * 16 // P
F = 1024
FT = F // P
E = 8
PAIRS = IMGS // 2
HG = 3
GROUPS = [(o, min(HG, H - o)) for o in range(0, H, HG)]
VW = HD + 1
CH = P
NCH = (TOK - E) // CH + E
EXP_W = KT * F + FT * D
EB_W = F + D
EPS = 1e-5
NEG = -1e30


def const_layout():
    at, out = 0, {}
    for name, w in (("ident", P), ("headmask", 4), ("cos", NT * HD), ("sin", NT * HD), ("before", P), ("ones", P),
                    ("vmask", H * VW), ("causal", 8 * SEQ), ("id64", 64), ("valid", NT), ("thr", E * NT),
                    ("upto", E * E), ("chunkno", NCH * E), ("eidx", E)):
        out[name] = (at, at + w)
        at += w
    return out, at


def shape_constants():
    lay, width = const_layout()
    c = np.zeros((P, width), np.float32)
    p = np.arange(P)

    def put(name, a):
        lo, hi = lay[name]
        c[:, lo:hi] = np.broadcast_to(a, (P,) + a.shape[1:]).reshape(P, hi - lo)

    put("ident", np.eye(P))
    put("headmask", ((p[:, None] % 64) // HD == np.arange(4)[None, :]).astype(np.float32))
    inv = 1.0 / 10000.0 ** (np.arange(0, HD, 2, dtype=np.float32) / np.float32(HD))
    pos = ((p[:, None] + P * np.arange(NT)[None, :]) % SEQ).astype(np.float32)
    ang = pos[:, :, None] * np.concatenate([inv, inv]).astype(np.float32)[None, None, :]
    sign = np.where(np.arange(HD) < HD // 2, -1.0, 1.0)
    put("cos", np.cos(ang))
    put("sin", np.sin(ang) * sign)
    put("before", (p[:, None] < p[None, :]).astype(np.float32))
    put("ones", np.ones((P, P)))
    vm = (p[:, None] // SEQ == np.arange(H)[None, :] % HG).astype(np.float32)
    put("vmask", np.repeat(vm, VW, axis=1))
    q = p % 64
    ca = np.where((q[:, None] < SEQ) & (np.arange(SEQ)[None, :] > q[:, None]), NEG, 0.0)
    put("causal", np.tile(ca, (1, 8)))
    put("id64", (q[:, None] == np.arange(64)[None, :]).astype(np.float32))
    put("valid", (p[:, None] + P * np.arange(NT)[None, :] < TOK).astype(np.float32))
    put("thr", np.tile(CH * np.arange(NT), E)[None, :])
    put("upto", (np.arange(E)[None, :] <= np.arange(E)[:, None]).astype(np.float32).reshape(1, -1))
    put("chunkno", np.repeat(np.arange(NCH), E)[None, :])
    put("eidx", np.arange(E)[None, :])
    return c


def tower(nc, xT_d, tokw_d, wqkv_d, wo_d, w1_d, w2_d, we_d, wr_d, rows_d, cols_d, eb_d, const_d, out_d):
    ctx = ExitStack()
    with ctx:
        def sb(name, shape, dt=F32):
            return ctx.enter_context(nc.sbuf_tensor(name, shape, dt))

        def sem(name):
            return ctx.enter_context(nc.semaphore(name))

        lay, cw = const_layout()
        const = sb("const", [P, cw])

        def cst(name):
            return const[:, lay[name][0]:lay[name][1]]

        ident = cst("ident")
        xs_dram = nc.dram_tensor("chunk_rows_in", [NCH * CH, D], F32, kind="Internal").ap()
        ys_dram = nc.dram_tensor("chunk_rows_out", [NCH * CH, D], F32, kind="Internal").ap()
        eb_dram = nc.dram_tensor("expert_bias_parts", [3, E * EB_W], BF16, kind="Internal").ap()
        v_dram = nc.dram_tensor("v_scratch", [TOK, D], F32, kind="Internal").ap()

        RES = 3
        we = sb("expert_w", [P, E * EXP_W])
        early = we[:, RES * EXP_W:E * EXP_W]
        at = [0]

        def carve(n):
            at[0] += n
            assert at[0] <= (E - RES) * EXP_W
            return early[:, at[0] - n:at[0]]

        vb = carve(IMGS * H * VW).rearrange("p (i o c) -> p i o c", i=IMGS, o=H)
        vrep = carve(IMGS * D).rearrange("p (i c) -> p i c", i=IMGS)
        tokw = carve(PATCH_K * D).rearrange("p (k n) -> p k n", k=PATCH_K)
        wqkv = carve(KT * 3 * D).rearrange("p (k n) -> p k n", k=KT)
        at[0] = 3 * EXP_W
        km_f = carve(KT * 4 * TOK)
        km = km_f.rearrange("p (t h n) -> p t h n", t=KT, h=4)
        xT = km_f[:, 0:PATCH_K * TOK].rearrange("p (k n) -> p k n", k=PATCH_K)
        hidT = km_f[:, 0:FT * TOK].rearrange("p (k n) -> p k n", k=FT)
        wo = sb("wo", [P, KT, D])
        w1 = carve(KT * F).rearrange("p (k n) -> p k n", k=KT)
        w2 = sb("w2", [P, FT, D])
        wr = sb("wr", [P, KT, E])
        rows = sb("rows", [P, 5 * D + E])
        cols = sb("cols", [P, 4 * KT + FT])
        res = sb("res", [P, NT, D])
        mid = sb("mid", [P, NT, D])
        x2 = carve(NT * D).rearrange("p (i c) -> p i c", i=NT)
        nrm = sb("nrm", [P, 2, D])
        nT = sb("nT", [P, KT, TOK])
        oT = nT
        bst = sb("bst", [P, NT, 6])
        mv = sb("mv", [P, NT, 2])
        nw = sb("nw", [P, 4, NT])
        nwi = sb("nwi", [P, 2, NT], I32)
        scr = sb("scr", [P, 2816 + E * EB_W // 2])
        qk = scr[:, 0:1024].rearrange("p (b n) -> p b n", b=2)
        ropec = scr[:, 1024:2048].rearrange("p (b n) -> p b n", b=2)
        ropes = scr[:, 2048:3072].rearrange("p (b n) -> p b n", b=2)
        vt = scr[:, 3072:3584].rearrange("p (b n) -> p b n", b=2)
        QTW = TOK + 32
        qT = scr[:, 3584:3584 + KT * QTW].rearrange("p (t n) -> p t n", t=KT)
        dif = scr[:, 0:1152].rearrange("p (b n) -> p b n", b=2)
        prob = scr[:, 1152:2304].rearrange("p (b n) -> p b n", b=2)
        pT = scr[:, 4800:4800 + 1536].rearrange("p (b g n) -> p b g n", b=2, g=len(GROUPS))
        on = scr[:, 6336:6848].rearrange("p (b n) -> p b n", b=2)
        xe = scr[:, 0:D]
        xeT = scr[:, D:2 * D].rearrange("p (k n) -> p k n", k=KT)
        eg = scr[:, 2 * D:2 * D + F]
        egT = scr[:, 2 * D + F:2 * D + 2 * F].rearrange("p (k n) -> p k n", k=FT)
        ey = scr[:, 2 * D + 2 * F:3 * D + 2 * F]
        ebr = scr[0:3, 2816:2816 + E * EB_W // 2].bitcast(BF16)
        yg = res
        zero = sb("zero", [P, D])
        EBP = E * EB_W // P
        ebf = sb("ebf", [P, 3, EBP])
        ebp = sb("ebp", [P, 3, EBP], BF16)
        lg = sb("lg", [P, NT, E])
        lmax = sb("lmax", [P, NT])
        first = sb("first", [P, NT, E])
        gate = sb("gate", [P, NT])
        onehot = sb("onehot", [P, NT, E])
        onehotb = sb("onehotb", [P, NT, E], BF16)
        beforeb = sb("beforeb", [P, P], BF16)
        onesb = sb("onesb", [P, P], BF16)
        cnt = sb("cnt", [P, 4, E])
        tmp = sb("tmp", [P, NCH * E])
        meta = sb("meta", [P, NCH + 1])
        metai = sb("metai", [P, NCH + 1], I32)
        row = sb("row", [P, NT])
        rowi = sb("rowi", [P, NT], I32)
        mx = sb("mx", [P, 2, H])
        rinv = sb("rinv", [P, 2, H])
        caus = sb("caus", [P, 8 * SEQ], BF16)
        id64 = sb("id64b", [P, 64], BF16)

        bank = [ctx.enter_context(nc.psum_tensor(f"bank{b}", [P, 512], F32)) for b in range(4)]
        bank45 = ctx.enter_context(nc.psum_tensor("bank45", [P, 1024], F32))
        bank += [bank45[:, 0:512], bank45[:, 512:1024]]
        bank += [ctx.enter_context(nc.psum_tensor(f"bank{b}", [P, 512], F32)) for b in (6, 7)]

        xt_in = [sem(f"xt_in{k}") for k in range(PATCH_K)]
        const_in = sem("const_in")
        rows_in = sem("rows_in")
        wqkv_in = sem("wqkv_in")
        mlp_in = sem("mlp_in")
        vt_out = [sem(f"vt_out{i}") for i in range(NT)]
        vrep_in = sem("vrep_in")
        out_st = sem("out_st")
        tok_mm = sem("tok_mm")
        res_ready = sem("res_ready")
        dve = sem("dve")
        pl = sem("pl")
        nrm_ready = [sem(f"nrm_ready{l}") for l in range(3)]
        nT_mm = [sem(f"nT_mm{l}") for l in range(3)]
        nT_ready = [sem(f"nT_ready{l}") for l in range(3)]
        qk_mm = sem("qk_mm")
        v_mm = sem("v_mm")
        qk_ready = sem("qk_ready")
        ropec_ready = sem("ropec_ready")
        ropes_ready = sem("ropes_ready")
        rope_ready = sem("rope_ready")
        vt_ready = sem("vt_ready")
        qkT_mm = sem("qkT_mm")
        qT_ready = sem("qT_ready")
        km_ready = sem("km_ready")
        qpad_ready = sem("qpad_ready")
        mask_ready = sem("mask_ready")
        vb_ready = sem("vb_ready")
        score_mm = sem("score_mm")
        dif_ready = sem("dif_ready")
        prob_ready = sem("prob_ready")
        pT_mm = sem("pT_mm")
        pT_ready = sem("pT_ready")
        av_mm = sem("av_mm")
        on_ready = sem("on_ready")
        oT_mm = sem("oT_mm")
        oT_ready = sem("oT_ready")
        mid_ready = sem("mid_ready")
        wo_mm = sem("wo_mm")
        x2_ready = sem("x2_ready")
        hx_ready = sem("hx_ready")
        up_mm = sem("up_mm")
        hid_ready = sem("hid_ready")
        down_mm = sem("down_mm")
        x3_ready = sem("x3_ready")
        we_in = [sem(f"we_in{e}") for e in range(E)]
        eb_in = sem("eb_in")
        eb_split = sem("eb_split")
        ebp_out = sem("ebp_out")
        ebr_in = sem("ebr_in")
        zero_ready = sem("zero_ready")
        rows_cleared = sem("rows_cleared")
        bf_ready = sem("bf_ready")
        logit_mm = sem("logit_mm")
        shift_ready = sem("shift_ready")
        expl_ready = sem("expl_ready")
        onehot_ready = sem("onehot_ready")
        rank_mm = sem("rank_mm")
        row_ready = sem("row_ready")
        meta_ready = sem("meta_ready")
        xs_out = sem("xs_out")
        xe_in = sem("xe_in")
        xeT_mm = sem("xeT_mm")
        xeT_ready = sem("xeT_ready")
        eup_mm, eg_ready, egT_mm, egT_ready = ([sem(f"{name}{s}") for s in range(2)] for name in
                                               ("eup_mm", "eg_ready", "egT_mm", "egT_ready"))
        ey_mm = sem("ey_mm")
        ey_ready = sem("ey_ready")
        ys_out = sem("ys_out")
        ey_room = sem("ey_room")
        yg_in = [sem(f"yg_in{i}") for i in range(NT)]
        y_ready = sem("y_ready")

        block = ctx.enter_context(nc.Block())

        def inverse_root(eng, link, var, lo, n, rows_):
            v, y, a, b = (nw[0:rows_, j, lo:lo + n] for j in range(4))
            link(eng.tensor_scalar(v, var, EPS, None, ALU.add))
            link(eng.tensor_scalar(nwi[0:rows_, 0, lo:lo + n], v.bitcast(I32), 1, None, ALU.logical_shift_right))
            link(eng.tensor_scalar(y.bitcast(I32), nwi[0:rows_, 0, lo:lo + n], -1, 0x5F3759DF, ALU.mult, ALU.add))
            for _ in range(3):
                link(eng.tensor_tensor(a, y, y, ALU.mult))
                link(eng.scalar_tensor_tensor(out=b, in0=a, scalar=-0.5, in1=v, op0=ALU.mult, op1=ALU.mult))
                link(eng.scalar_tensor_tensor(out=y, in0=b, scalar=1.5, in1=y, op0=ALU.add, op1=ALU.mult))
            return y

        def chunks_in_use(eng):
            eng.wait_ge(meta_ready, 2)
            return eng.value_load(metai[0:1, NCH:NCH + 1], min_val=1, max_val=NCH)

        @block.sync
        def _(sp):
            for k in range(PATCH_K):
                sp.dma_start(xT[:, k, :], xT_d[:, k, :]).then_inc(xt_in[k], 16)
                sp.dma_start(tokw[:, k, :], tokw_d[:, k, :]).then_inc(xt_in[k], 16)
            sp.dma_start(const[:, :], const_d).then_inc(const_in, 16)
            sp.dma_start(cols[:, :], cols_d).then_inc(const_in, 16)
            sp.dma_start(rows[:, :], rows_d.broadcast_to((P, 5 * D + E))).then_inc(rows_in, 16)
            sp.dma_start(wqkv[:, :, :], wqkv_d).then_inc(wqkv_in, 16)
            sp.dma_start(wo[:, :, :], wo_d).then_inc(mlp_in, 16)
            sp.dma_start(w1[:, :, :], w1_d).then_inc(mlp_in, 16)
            sp.dma_start(w2[:, :, :], w2_d).then_inc(mlp_in, 16)
            sp.dma_start(wr[:, :, :], wr_d).then_inc(mlp_in, 16)
            sp.dma_start(ebf[:, 0, :], eb_d).then_inc(eb_in, 16)
            sp.wait_ge(zero_ready, 1)
            for chunk_rows in (xs_dram, ys_dram):
                sp.dma_start(chunk_rows.rearrange("(c p) d -> p c d", p=CH),
                             zero[:, :].rearrange("p (o d) -> p o d", o=1).broadcast_to((P, NCH, D)))\
                    .then_inc(rows_cleared, 16)
            for e in range(RES):
                sp.dma_start(we[:, e * EXP_W:(e + 1) * EXP_W], we_d[e]).then_inc(we_in[e], 16)
            for i, (t0, n) in enumerate(TILES):
                sp.wait_ge(vt_ready, i + 1)
                sp.dma_start(v_dram[t0:t0 + n, :], vt[0:n, i % 2, :]).then_inc(vt_out[i], 16)
            for i in range(NT):
                sp.wait_ge(vt_out[i], 16)
            for j in range(HG):
                sp.dma_start(vrep[SEQ * j:SEQ * (j + 1), :, :],
                             v_dram.rearrange("(i k) c -> k i c", k=SEQ)).then_inc(vrep_in, 16)
            sp.wait_ge(eb_split, 3)
            sp.dma_start(eb_dram.rearrange("s (p c) -> p s c", p=P), ebp[:, :, :]).then_inc(ebp_out, 16)
            sp.wait_ge(av_mm, PAIRS)
            sp.wait_ge(ebp_out, 16)
            for e in range(RES, 6):
                sp.dma_start(we[:, e * EXP_W:(e + 1) * EXP_W], we_d[e]).then_inc(we_in[e], 16)
            sp.wait_ge(oT_ready, PAIRS)
            sp.dma_start(ebr, eb_dram).then_inc(ebr_in, 16)
            sp.wait_ge(down_mm, NT)
            sp.wait_ge(hx_ready, NT)
            for e in range(6, E):
                sp.dma_start(we[:, e * EXP_W:(e + 1) * EXP_W], we_d[e]).then_inc(we_in[e], 16)
            n_chunks = chunks_in_use(sp)
            sp.wait_ge(xs_out, 16 * NT)
            sp.dma_start(xe, xs_dram[0:CH, :]).then_inc(xe_in, 16)
            with sp.Fori(1, NCH) as c:
                with sp.If(c < n_chunks):
                    sp.wait_ge(xeT_mm, c)
                    sp.dma_start(xe, xs_dram[ds(c * CH, CH), :]).then_inc(xe_in, 16)
            for i, (t0, n) in enumerate(TILES):
                sp.wait_ge(y_ready, i + 1)
                sp.dma_start(out_d[t0:t0 + n, :], yg[0:n, i, :]).then_inc(out_st, 16)
            sp.wait_ge(out_st, 16 * NT)

        @block.tensor
        def _(pe):
            def transpose_tile(l, i):
                t0, n = TILES[i]
                b = bank[5 + i % 2]
                pe.wait_ge(nrm_ready[l], i + 1)
                if i >= 2:
                    pe.wait_ge(nT_ready[l], i - 1)
                for k in range(KT):
                    last = pe.transpose(b[:, k * P:k * P + n], nrm[0:n, i % 2, k * P:(k + 1) * P], ident[0:n, 0:n])
                last.then_inc(nT_mm[l], 1)

            for k in range(PATCH_K):
                pe.wait_ge(xt_in[k], 32)
                for i, (t0, n) in enumerate(TILES):
                    last = pe.matmul(bank[i][0:n, 0:D], xT[:, k, t0:t0 + n], tokw[:, k, :],
                                     start=(k == 0), stop=(k == PATCH_K - 1))
                    if k == PATCH_K - 1:
                        last.then_inc(tok_mm, 1)
            pe.wait_ge(const_in, 32)

            def project(i):
                t0, n = TILES[i]
                pe.wait_ge(nT_ready[0], i + 1)
                if i == 0:
                    pe.wait_ge(wqkv_in, 16)
                if i < 2:
                    pe.wait_ge(res_ready, 2 * i + 2)
                if i >= 2:
                    pe.wait_ge(qk_ready, i - 1)
                    pe.wait_ge(vt_ready, i - 1)
                for k in range(KT):
                    last = pe.matmul(bank[2 * (i % 2)][0:n, :], nT[:, k, t0:t0 + n], wqkv[:, k, 0:2 * D],
                                     start=(k == 0), stop=(k == KT - 1))
                last.then_inc(qk_mm, 1)
                for k in range(KT):
                    last = pe.matmul(bank[2 * (i % 2) + 1][0:n, 0:D], nT[:, k, t0:t0 + n], wqkv[:, k, 2 * D:3 * D],
                                     start=(k == 0), stop=(k == KT - 1))
                last.then_inc(v_mm, 1)

            def turn_qk(i):
                t0, n = TILES[i]
                pe.wait_ge(rope_ready, i + 1)
                if i == 0:
                    pe.wait_ge(res_ready, NT)
                else:
                    pe.wait_ge(qT_ready, i)
                    pe.wait_ge(km_ready, i)
                for j in range(4):
                    last = pe.transpose(bank[4 + 3 * (j // 2)][:, (j % 2) * P:(j % 2) * P + n], ropec[0:n, i % 2, j * P:(j + 1) * P],
                                        ident[0:n, 0:n])
                last.then_inc(qkT_mm, 1)

            transpose_tile(0, 0)
            for i in range(NT):
                if i + 1 < NT:
                    transpose_tile(0, i + 1)
                project(i)
                if i >= 1:
                    turn_qk(i - 1)
            turn_qk(NT - 1)

            def scores(p):
                if p == 0:
                    pe.wait_ge(qT_ready, NT)
                    pe.wait_ge(km_ready, NT)
                    pe.wait_ge(qpad_ready, 1)
                    pe.wait_ge(mask_ready, 2)
                    pe.wait_ge(vt_ready, NT)
                if p >= 2:
                    pe.wait_ge(dif_ready, p - 1)
                for im in range(2):
                    q0 = (2 * p + im) * SEQ
                    for half in range(2):
                        s = bank[2 * (p % 2) + half][64 * im:64 * im + 64, :]
                        r = slice(64 * half, 64 * half + 64)
                        pe.matmul(s[:, 0:8 * SEQ], id64[r, :], caus[r, :], start=True, stop=False,
                                  skip_group_check=True)
                        for t in range(KT):
                            last = pe.matmul(s[:, t * 4 * SEQ:(t + 1) * 4 * SEQ], qT[r, t, q0:q0 + 64],
                                             km[r, t, :, q0:q0 + SEQ], start=False, stop=True, skip_group_check=True)
                last.then_inc(score_mm, 1)

            def turn_probs(p):
                pe.wait_ge(prob_ready, p + 1)
                if p >= 1:
                    pe.wait_ge(pT_ready, p)
                else:
                    pe.wait_ge(nT_ready[0], NT)
                for g, (o, nh) in enumerate(GROUPS):
                    last = pe.transpose(bank45[0:nh * SEQ, g * P:(g + 1) * P],
                                        prob[:, p % 2, o * SEQ:(o + nh) * SEQ], ident)
                last.then_inc(pT_mm, 1)

            def values(p):
                pe.wait_ge(pT_ready, p + 1)
                pe.wait_ge(vb_ready, p + 1)
                if p >= 1:
                    pe.wait_ge(on_ready, p)
                for im in range(2):
                    for g, (o, nh) in enumerate(GROUPS):
                        last = pe.matmul(bank[6][64 * im:64 * im + 64, o * VW:(o + nh) * VW],
                                         pT[0:nh * SEQ, p % 2, g, 64 * im:64 * im + 64],
                                         vb[0:nh * SEQ, 2 * p + im, o:o + nh, :], start=True, stop=True)
                last.then_inc(av_mm, 1)

            def turn_out(p):
                pe.wait_ge(on_ready, p + 1)
                if p >= 1:
                    pe.wait_ge(oT_ready, p)
                for k in range(KT):
                    last = pe.transpose(bank[7][:, k * P:(k + 1) * P], on[:, p % 2, k * P:(k + 1) * P], ident)
                last.then_inc(oT_mm, 1)

            for p in range(PAIRS + 3):
                if p < PAIRS:
                    scores(p)
                if 1 <= p <= PAIRS:
                    turn_probs(p - 1)
                if 2 <= p <= PAIRS + 1:
                    values(p - 2)
                if 3 <= p:
                    turn_out(p - 3)

            def out_proj(i):
                t0, n = TILES[i]
                if i == 0:
                    pe.wait_ge(mlp_in, 64)
                    pe.wait_ge(dif_ready, PAIRS)
                    pe.wait_ge(pT_ready, PAIRS)
                    pe.wait_ge(oT_ready, PAIRS)
                for k in range(KT):
                    last = pe.matmul(bank[i][0:n, 0:D], oT[:, k, t0:t0 + n], wo[:, k, :],
                                     start=(k == 0), stop=(k == KT - 1))
                last.then_inc(wo_mm, 1)

            for i in range(NT):
                out_proj(i)
            for i in range(NT):
                transpose_tile(1, i)

            HT = TOK // 2
            for j in range(FT):
                if j == 0:
                    pe.wait_ge(nT_ready[1], NT)
                    pe.wait_ge(x2_ready, NT)
                if j >= 2:
                    pe.wait_ge(hid_ready, j - 1)
                for s in range(2):
                    for k in range(KT):
                        last = pe.matmul(bank[2 * (j % 2) + s][:, 0:HT], w1[:, k, j * P:(j + 1) * P],
                                         nT[:, k, s * HT:(s + 1) * HT], start=(k == 0), stop=(k == KT - 1))
                last.then_inc(up_mm, 1)
            for i, (t0, n) in enumerate(TILES):
                if i == 0:
                    pe.wait_ge(hid_ready, FT)
                for j in range(FT):
                    last = pe.matmul(bank[(4 + i) % 8][0:n, 0:D], hidT[:, j, t0:t0 + n], w2[:, j, :],
                                     start=(j == 0), stop=(j == FT - 1))
                last.then_inc(down_mm, 1)

            for i in range(NT):
                t0, n = TILES[i]
                pe.wait_ge(x3_ready, i + 1)
                if i >= 2:
                    pe.wait_ge(nT_ready[2], i - 1)
                for k in range(KT):
                    last = pe.transpose(bank[1 + i % 2][:, k * P:k * P + n], mid[0:n, i, k * P:(k + 1) * P],
                                        ident[0:n, 0:n])
                last.then_inc(nT_mm[2], 1)
            for i, (t0, n) in enumerate(TILES):
                pe.wait_ge(nT_ready[2], i + 1)
                for k in range(KT):
                    last = pe.matmul(bank[3][0:n, i * E:(i + 1) * E], nT[:, k, t0:t0 + n], wr[:, k, :],
                                     start=(k == 0), stop=(k == KT - 1))
            last.then_inc(logit_mm, 1)
            pe.wait_ge(onehot_ready, 1)
            pe.wait_ge(bf_ready, 2)
            for i in range(NT + 1):
                for j in range(min(i + 1, NT)):
                    last = pe.matmul(bank[4][:, i * E:(i + 1) * E], beforeb[:, :] if j == i else onesb[:, :],
                                     onehotb[:, j, :], start=(j == 0), stop=(j == min(i, NT - 1)))
            last.then_inc(rank_mm, 1)

            def turn_rows(c):
                pe.wait_ge(xe_in, 16 * (c + 1))
                for k in range(KT):
                    last = pe.transpose(bank[5][:, k * P:(k + 1) * P], xe[:, k * P:(k + 1) * P], ident)
                last.then_inc(xeT_mm, 1)

            def expert_up(c, e):
                pe.wait_ge(xeT_ready, c + 1)
                for s in range(2):
                    pe.matmul(bank[s][:, :], onesb[0:3, :], ebr[:, ds(e * EB_W + s * 512, 512)],
                              start=True, stop=False)
                    for k in range(KT):
                        last = pe.matmul(bank[s][:, :], xeT[:, k, :], we[:, ds(e * EXP_W + k * F + s * 512, 512)],
                                         start=False, stop=(k == KT - 1))
                    last.then_inc(eup_mm[s], 1)

            def turn_hidden(done):
                for s in range(2):
                    pe.wait_ge(eg_ready[s], done)
                    for j in range(4 * s, 4 * s + 4):
                        last = pe.transpose(bank[2 + s][:, (j % 4) * P:(j % 4 + 1) * P], eg[:, j * P:(j + 1) * P],
                                            ident)
                    last.then_inc(egT_mm[s], 1)

            def expert_down(done, e):
                pe.wait_ge(egT_ready[0], done)
                pe.matmul(bank[6][:, 0:D], onesb[0:3, :], ebr[:, ds(e * EB_W + F, D)], start=True, stop=False)
                for j in range(FT):
                    if j == 4:
                        pe.wait_ge(egT_ready[1], done)
                    last = pe.matmul(bank[6][:, 0:D], egT[:, j, :], we[:, ds(e * EXP_W + KT * F + j * D, D)],
                                     start=False, stop=(j == FT - 1))
                last.then_inc(ey_mm, 1)

            n_chunks = chunks_in_use(pe)

            def expert_of(c):
                return pe.value_load(metai[0:1, ds(c, 1)], min_val=0, max_val=E - 1)

            pe.wait_ge(ebr_in, 16)
            for e in range(E):
                pe.wait_ge(we_in[e], 16)
            turn_rows(0)
            expert_up(0, expert_of(0))
            with pe.Fori(1, NCH) as c:
                with pe.If(c < n_chunks):
                    turn_rows(c)
                    turn_hidden(c)
                    expert_up(c, expert_of(c))
                    expert_down(c, expert_of(c - 1))
            turn_hidden(n_chunks)
            expert_down(n_chunks, expert_of(n_chunks - 1))

        @block.vector
        def _(v):
            count = [0]

            def link(ins):
                count[0] += 1
                ins.then_inc(dve, 1)
                v.wait_ge(dve, count[0])

            def layer_stats(src, i, n):
                link(v.bn_stats(bst[0:n, i, :], src))
                link(v.bn_aggr(mv[0:n, i, :], bst[0:n, i, :]))
                return inverse_root(v, link, mv[0:n, i, 1:2], i, 1, n)

            def normalise(dst, src, i, n, inv, done):
                v.tensor_scalar(dst, src, mv[0:n, i, 0:1], inv, ALU.subtract, ALU.mult).then_inc(done, 1)

            def affine_T(l, i, g, b):
                t0, n = TILES[i]
                v.wait_ge(nT_mm[l], i + 1)
                for k in range(KT):
                    last = v.tensor_scalar(nT[:, k, t0:t0 + n], bank[5 + i % 2][:, k * P:k * P + n],
                                           cols[:, g * KT + k:g * KT + k + 1], cols[:, b * KT + k:b * KT + k + 1],
                                           ALU.mult, ALU.add)
                last.then_inc(nT_ready[l], 1)

            def norm1(i):
                t0, n = TILES[i]
                v.wait_ge(res_ready, i + 1)
                inv = layer_stats(res[0:n, i, :], i, n)
                if i >= 2:
                    v.wait_ge(nT_mm[0], i - 1)
                normalise(nrm[0:n, i % 2, :], res[0:n, i, :], i, n, inv, nrm_ready[0])

            def empty_qkv(i):
                t0, n = TILES[i]
                v.wait_ge(qk_mm, i + 1)
                if i == 0:
                    v.wait_ge(rows_in, 16)
                if i >= 2:
                    v.wait_ge(ropec_ready, i - 1)
                v.tensor_tensor(qk[0:n, i % 2, :], bank[2 * (i % 2)][0:n, :], rows[0:n, 0:2 * D],
                                ALU.add).then_inc(qk_ready, 1)
                v.wait_ge(v_mm, i + 1)
                if i >= 2:
                    v.wait_ge(vt_out[i - 2], 16)
                v.tensor_tensor(vt[0:n, i % 2, :], bank[2 * (i % 2) + 1][0:n, 0:D], rows[0:n, 2 * D:3 * D],
                                ALU.add).then_inc(vt_ready, 1)
                v.wait_ge(qk_ready, i + 1)
                if i >= 2:
                    v.wait_ge(rope_ready, i - 1)
                q4 = qk[0:n, i % 2, :].rearrange("p (h a c) -> p h a c", a=2, c=HD // 2)
                s4 = ropes[0:n, i % 2, :].rearrange("p (h a c) -> p h a c", a=2, c=HD // 2)
                sn = cst("sin")[0:n, i * HD:(i + 1) * HD].rearrange("p (o a c) -> p o a c", o=1, a=2)
                for a in range(2):
                    last = v.tensor_tensor(s4[:, :, a, :], q4[:, :, 1 - a, :],
                                           sn[:, :, a, :].broadcast_to((n, 2 * H, HD // 2)), ALU.mult)
                last.then_inc(ropes_ready, 1)

            def mask_keys(i):
                t0, n = TILES[i]
                v.wait_ge(qkT_mm, i + 1)
                for t in range(KT):
                    src = bank[7][:, t * P:t * P + n].rearrange("p (o n) -> p o n", o=1).broadcast_to((P, 4, n))
                    hm = cst("headmask").rearrange("p (h o) -> p h o", o=1).broadcast_to((P, 4, n))
                    last = v.tensor_tensor(km[:, t, :, t0:t0 + n], src, hm, ALU.mult)
                last.then_inc(km_ready, 1)

            for i in range(NT):
                norm1(i)
                if i >= 1:
                    if i == 1:
                        v.wait_ge(const_in, 32)
                    affine_T(0, i - 1, 0, 1)
                if i >= 2:
                    empty_qkv(i - 2)
                if i >= 3:
                    mask_keys(i - 3)
            affine_T(0, NT - 1, 0, 1)
            empty_qkv(NT - 2)
            mask_keys(NT - 3)
            empty_qkv(NT - 1)
            mask_keys(NT - 2)
            mask_keys(NT - 1)

            def soft_in(p):
                v.wait_ge(score_mm, p + 1)
                if p == 0:
                    v.wait_ge(qkT_mm, NT)
                    v.wait_ge(ropec_ready, NT)
                if p >= 2:
                    v.wait_ge(prob_ready, p - 1)
                for half in range(2):
                    s = bank[2 * (p % 2) + half][:, 0:8 * SEQ].rearrange("p (h k) -> p h k", k=SEQ)
                    link(v.tensor_reduce(mx[:, p % 2, 8 * half:8 * half + 8], s, AX, ALU.max))
                for half in range(2):
                    s = bank[2 * (p % 2) + half][:, 0:8 * SEQ].rearrange("p (h k) -> p h k", k=SEQ)
                    m = mx[:, p % 2, 8 * half:8 * half + 8].rearrange("p (h o) -> p h o", o=1).broadcast_to((P, 8, SEQ))
                    d = dif[:, p % 2, half * 8 * SEQ:(half + 1) * 8 * SEQ].rearrange("p (h k) -> p h k", k=SEQ)
                    last = v.tensor_tensor(d, s, m, ALU.subtract)
                last.then_inc(dif_ready, 1)

            def soft_out(p):
                v.wait_ge(av_mm, p + 1)
                o3 = bank[6][:, 0:H * VW].rearrange("p (o c) -> p o c", c=VW)
                link(v.reciprocal(rinv[:, p % 2, :], o3[:, :, HD]))
                if p >= 2:
                    v.wait_ge(oT_mm, p - 1)
                v.tensor_tensor(on[:, p % 2, :].rearrange("p (o c) -> p o c", c=HD), o3[:, :, 0:HD],
                                rinv[:, p % 2, :].rearrange("p (h o) -> p h o", o=1).broadcast_to((P, H, HD)),
                                ALU.mult).then_inc(on_ready, 1)

            for p in range(PAIRS + 2):
                if p < PAIRS:
                    soft_in(p)
                if p >= 2:
                    soft_out(p - 2)

            for i, (t0, n) in enumerate(TILES):
                v.wait_ge(wo_mm, i + 1)
                v.wait_ge(mid_ready, i + 1)
                v.tensor_tensor(x2[0:n, i, :], bank[i][0:n, 0:D], mid[0:n, i, :], ALU.add).then_inc(x2_ready, 1)
                v.wait_ge(x2_ready, i + 1)
                inv = layer_stats(x2[0:n, i, :], i, n)
                if i >= 2:
                    v.wait_ge(nT_mm[1], i - 1)
                normalise(nrm[0:n, i % 2, :], x2[0:n, i, :], i, n, inv, nrm_ready[1])
                if i >= 1:
                    affine_T(1, i - 1, 2, 3)
            affine_T(1, NT - 1, 2, 3)

            for i, (t0, n) in enumerate(TILES):
                v.wait_ge(down_mm, i + 1)
                v.wait_ge(hx_ready, i + 1)
                link(v.tensor_tensor(mid[0:n, i, :], bank[(4 + i) % 8][0:n, 0:D], res[0:n, i, :], ALU.add))
                inv = layer_stats(mid[0:n, i, :], i, n)
                normalise(mid[0:n, i, :], mid[0:n, i, :], i, n, inv, x3_ready)

            lgb = [P, NT, E]
            link(v.memset(lg[:, :, :], 0.0))
            for i, (t0, n) in enumerate(TILES):
                v.wait_ge(nT_mm[2], i + 1)
                v.tensor_copy(nT[:, :, t0:t0 + n],
                              bank[1 + i % 2][:, 0:2 * P].rearrange("p (t n) -> p t n", t=KT)[:, :, 0:n])\
                    .then_inc(nT_ready[2], 1)
            v.wait_ge(logit_mm, 1)
            full = NT - 1
            last_n = TILES[full][1]
            br = rows[:, 5 * D:5 * D + E].rearrange("p (o e) -> p o e", o=1)
            link(v.tensor_tensor(lg[:, 0:full, :], bank[3][:, 0:full * E].rearrange("p (i e) -> p i e", e=E),
                                 br.broadcast_to((P, full, E)), ALU.add))
            link(v.tensor_tensor(lg[0:last_n, full, :], bank[3][0:last_n, full * E:NT * E], rows[0:last_n, 5 * D:],
                                 ALU.add))
            link(v.tensor_reduce(lmax[:, :], lg[:, :, :], AX, ALU.max))
            top = lmax[:, :].rearrange("p (i o) -> p i o", o=1).broadcast_to(lgb)
            link(v.tensor_tensor(first[:, :, :], lg[:, :, :], top, ALU.is_equal))
            v.tensor_tensor(lg[:, :, :], lg[:, :, :], top, ALU.subtract).then_inc(shift_ready, 1)
            eidx = cst("eidx").rearrange("p (o e) -> p o e", o=1).broadcast_to(lgb)
            link(v.scalar_tensor_tensor(out=first[:, :, :], in0=first[:, :, :], scalar=-float(E), in1=eidx,
                                        op0=ALU.mult, op1=ALU.add))
            link(v.tensor_reduce(row[:, :], first[:, :, :], AX, ALU.min))
            link(v.tensor_tensor(onehot[:, :, :], first[:, :, :],
                                 row[:, :].rearrange("p (i o) -> p i o", o=1).broadcast_to(lgb), ALU.is_equal))
            valid = cst("valid").rearrange("p (i o) -> p i o", o=1).broadcast_to(lgb)
            v.tensor_tensor(onehotb[:, :, :], onehot[:, :, :], valid, ALU.mult).then_inc(onehot_ready, 1)
            v.wait_ge(expl_ready, 1)
            link(v.tensor_reduce(gate[:, :], lg[:, :, :], AX, ALU.add))
            link(v.reciprocal(gate[:, :], gate[:, :]))

            v.wait_ge(rank_mm, 1)
            v.wait_ge(onehot_ready, 1)
            ranks = bank[4][:, 0:NT * E].rearrange("p (i e) -> p i e", e=E)
            link(v.tensor_copy(cnt[:, 0, :], bank[4][:, NT * E:(NT + 1) * E]))
            t5 = tmp[:, 0:E * NT].rearrange("p (e j) -> p e j", e=E)
            link(v.tensor_tensor(t5, cnt[:, 0, :].rearrange("p (e o) -> p e o", o=1).broadcast_to((P, E, NT)),
                                 cst("thr").rearrange("p (e j) -> p e j", e=E), ALU.is_gt))
            link(v.tensor_reduce(cnt[:, 1, :], t5, AX, ALU.add))
            t8 = tmp[:, 0:E * E].rearrange("p (a b) -> p a b", a=E)
            link(v.tensor_tensor(t8, cnt[:, 1, :].rearrange("p (o e) -> p o e", o=1).broadcast_to((P, E, E)),
                                 cst("upto").rearrange("p (a b) -> p a b", a=E), ALU.mult))
            link(v.tensor_reduce(cnt[:, 2, :], t8, AX, ALU.add))
            link(v.tensor_tensor(cnt[:, 3, :], cnt[:, 2, :], cnt[:, 1, :], ALU.subtract))
            link(v.scalar_tensor_tensor(out=first[:, :, :],
                                        in0=cnt[:, 3, :].rearrange("p (o e) -> p o e", o=1).broadcast_to(lgb),
                                        scalar=float(CH), in1=ranks, op0=ALU.mult, op1=ALU.add))
            link(v.tensor_tensor(first[:, :, :], first[:, :, :], onehot[:, :, :], ALU.mult))
            link(v.tensor_reduce(row[:, :], first[:, :, :], AX, ALU.add))
            v.tensor_copy(rowi[:, :], row[:, :]).then_inc(row_ready, 1)
            tc = tmp[:, :].rearrange("p (c e) -> p c e", e=E)
            link(v.tensor_tensor(tc, cnt[:, 2, :].rearrange("p (o e) -> p o e", o=1).broadcast_to((P, NCH, E)),
                                 cst("chunkno").rearrange("p (c e) -> p c e", e=E), ALU.is_le))
            link(v.tensor_reduce(meta[:, 0:NCH], tc, AX, ALU.add))
            v.tensor_copy(metai[:, 0:NCH], meta[:, 0:NCH]).then_inc(meta_ready, 1)
            v.tensor_copy(metai[:, NCH:NCH + 1], cnt[:, 2, E - 1:E]).then_inc(meta_ready, 1)

            n_chunks = chunks_in_use(v)

            def keep_rows(c):
                v.wait_ge(xeT_mm, c + 1)
                v.tensor_copy(xeT[:, :, :].rearrange("p k n -> p (k n)"), bank[5][:, 0:2 * P]).then_inc(xeT_ready, 1)

            def keep_hidden(done):
                for s in range(2):
                    v.wait_ge(egT_mm[s], done)
                    v.tensor_copy(egT[:, 4 * s:4 * s + 4, :].rearrange("p k n -> p (k n)"), bank[2 + s][:, :])\
                        .then_inc(egT_ready[s], 1)

            def keep_y(done):
                v.wait_ge(ey_mm, done)
                v.wait_ge(ey_room, done)
                v.tensor_copy(ey, bank[6][:, 0:D]).then_inc(ey_ready, 1)

            v.sem_inc(ey_room, 1)
            keep_rows(0)
            with v.Fori(1, NCH) as c:
                with v.If(c < n_chunks):
                    keep_rows(c)
                    keep_hidden(c)
                    keep_y(c)
            keep_hidden(n_chunks)
            keep_y(n_chunks)

            for i, (t0, n) in enumerate(TILES):
                v.wait_ge(yg_in[i], 16)
                link(v.scalar_tensor_tensor(out=yg[0:n, i, :], in0=yg[0:n, i, :], scalar=gate[0:n, i:i + 1],
                                            in1=mid[0:n, i, :], op0=ALU.mult, op1=ALU.add))
                inv = layer_stats(yg[0:n, i, :], i, n)
                normalise(yg[0:n, i, :], yg[0:n, i, :], i, n, inv, y_ready)

        @block.scalar
        def _(a):
            for i, (t0, n) in enumerate(TILES):
                a.wait_ge(tok_mm, i + 1)
                a.activation(res[0:n, i, :], bank[i][0:n, 0:D], ACT.Copy).then_inc(res_ready, 1)
            for i, (t0, n) in enumerate(TILES):
                a.wait_ge(qkT_mm, i + 1)
                a.activation(qT[:, :, t0:t0 + n], bank[4][:, 0:2 * P].rearrange("p (t n) -> p t n", t=KT)[:, :, 0:n],
                             ACT.Copy).then_inc(qT_ready, 1)

            def exps(p):
                a.wait_ge(dif_ready, p + 1)
                if p == 0:
                    a.wait_ge(rope_ready, NT)
                    a.wait_ge(qkT_mm, NT)
                if p >= 2:
                    a.wait_ge(pT_mm, p - 1)
                a.activation(prob[:, p % 2, :], dif[:, p % 2, :], ACT.Exp, scale=float(HD) ** -0.5)\
                    .then_inc(prob_ready, 1)

            def copy_pT(p):
                a.wait_ge(pT_mm, p + 1)
                if p >= 2:
                    a.wait_ge(av_mm, p - 1)
                full = len(GROUPS) - 1
                a.activation(pT[0:HG * SEQ, p % 2, 0:full, :].rearrange("p g n -> p (g n)"),
                             bank45[0:HG * SEQ, 0:full * P], ACT.Copy)
                nh = GROUPS[full][1]
                a.activation(pT[0:nh * SEQ, p % 2, full, :], bank45[0:nh * SEQ, full * P:(full + 1) * P],
                             ACT.Copy).then_inc(pT_ready, 1)

            def copy_oT(p):
                a.wait_ge(oT_mm, p + 1)
                src = bank[7][:, 0:2 * P].rearrange("p (t i q) -> p t i q", t=KT, i=2)[:, :, :, 0:SEQ]
                dst = oT[:, :, 2 * p * SEQ:(2 * p + 2) * SEQ].rearrange("p t (i q) -> p t i q", i=2)
                a.activation(dst, src, ACT.Copy).then_inc(oT_ready, 1)

            for p in range(PAIRS + 3):
                if p < PAIRS:
                    exps(p)
                if 1 <= p <= PAIRS:
                    copy_pT(p - 1)
                if p >= 3:
                    copy_oT(p - 3)

            HT = TOK // 2
            for j in range(FT):
                a.wait_ge(up_mm, j + 1)
                for s in range(2):
                    last = a.activation(hidT[:, j, s * HT:(s + 1) * HT], bank[2 * (j % 2) + s][:, 0:HT], ACT.Gelu,
                                        bias=cols[:, 4 * KT + j:4 * KT + j + 1])
                last.then_inc(hid_ready, 1)

            a.wait_ge(shift_ready, 1)
            a.activation(lg[:, :, :], lg[:, :, :], ACT.Exp).then_inc(expl_ready, 1)

            n_chunks = chunks_in_use(a)

            def gelu(c):
                for s in range(2):
                    a.wait_ge(eup_mm[s], c + 1)
                    a.activation(eg[:, s * 512:(s + 1) * 512], bank[s][:, :], ACT.Gelu).then_inc(eg_ready[s], 1)

            gelu(0)
            with a.Fori(1, NCH) as c:
                with a.If(c < n_chunks):
                    gelu(c)

        @block.gpsimd
        def _(g):
            g.memset(zero[:, :], 0.0).then_inc(zero_ready, 1)
            g.wait_ge(const_in, 32)
            g.tensor_copy(beforeb[:, :], cst("before")).then_inc(bf_ready, 1)
            g.tensor_copy(onesb[:, :], cst("ones")).then_inc(bf_ready, 1)
            g.tensor_copy(caus[:, :], cst("causal")).then_inc(mask_ready, 1)
            g.tensor_copy(id64[:, :], cst("id64")).then_inc(mask_ready, 1)
            g.memset(qT[:, :, TOK:QTW], 0.0).then_inc(qpad_ready, 1)
            for i, (t0, n) in enumerate(TILES):
                g.wait_ge(qk_ready, i + 1)
                if i >= 2:
                    g.wait_ge(qkT_mm, i - 1)
                cs = cst("cos")[0:n, i * HD:(i + 1) * HD].rearrange("p (o c) -> p o c", o=1).broadcast_to((n, 2 * H, HD))
                g.tensor_tensor(ropec[0:n, i % 2, :].rearrange("p (h c) -> p h c", c=HD),
                                qk[0:n, i % 2, :].rearrange("p (h c) -> p h c", c=HD), cs, ALU.mult)\
                    .then_inc(ropec_ready, 1)
                g.wait_ge(ropec_ready, i + 1)
                g.wait_ge(ropes_ready, i + 1)
                g.tensor_tensor(ropec[0:n, i % 2, :], ropec[0:n, i % 2, :], ropes[0:n, i % 2, :],
                                ALU.add).then_inc(rope_ready, 1)
            g.wait_ge(eb_in, 16)
            for s in range(3):
                g.tensor_copy(ebp[:, s, :], ebf[:, s, :]).then_inc(eb_split, 1)
                g.wait_ge(eb_split, s + 1)
                if s < 2:
                    g.tensor_tensor(ebf[:, s + 1, :], ebf[:, s, :], ebp[:, s, :], ALU.subtract).then_inc(pl, 1)
                    g.wait_ge(pl, s + 1)
            R = HG * SEQ
            vm = cst("vmask")[0:R, :].rearrange("p (i o c) -> p i o c", i=1, c=VW)
            g.tensor_copy(vb[0:R, :, :, HD], vm[:, :, :, HD].broadcast_to((R, IMGS, H))).then_inc(pl, 1)
            g.wait_ge(vrep_in, 16 * HG)
            for p in range(PAIRS):
                src = vrep[0:R, 2 * p:2 * p + 2, :].rearrange("p i (o c) -> p i o c", c=HD)
                g.tensor_tensor(vb[0:R, 2 * p:2 * p + 2, :, 0:HD], src, vm[:, :, :, 0:HD].broadcast_to((R, 2, H, HD)), ALU.mult)\
                    .then_inc(vb_ready, 1)
            for i, (t0, n) in enumerate(TILES):
                g.wait_ge(res_ready, i + 1)
                g.tensor_tensor(mid[0:n, i, :], res[0:n, i, :], rows[0:n, 3 * D:4 * D], ALU.add).then_inc(mid_ready, 1)
            for i, (t0, n) in enumerate(TILES):
                g.wait_ge(x2_ready, i + 1)
                g.tensor_tensor(res[0:n, i, :], res[0:n, i, :], x2[0:n, i, :], ALU.add).then_inc(pl, 1)
                g.wait_ge(pl, i + 4)
                g.tensor_tensor(res[0:n, i, :], res[0:n, i, :], rows[0:n, 4 * D:5 * D], ALU.add).then_inc(hx_ready, 1)
            g.wait_ge(row_ready, 1)
            g.wait_ge(rows_cleared, 32)
            for i, (t0, n) in enumerate(TILES):
                g.indirect_dma_start(xs_dram, bass.IndirectOffsetOnAxis(rowi[0:n, i:i + 1], 0), mid[0:n, i, :], None)\
                    .then_inc(xs_out, 16)
            n_chunks = chunks_in_use(g)
            g.wait_ge(ey_ready, 1)
            g.dma_start(ys_dram[0:CH, :], ey).then_inc(ys_out, 16)
            g.wait_ge(ys_out, 16)
            g.sem_inc(ey_room, 1)
            with g.Fori(1, NCH) as c:
                with g.If(c < n_chunks):
                    g.wait_ge(ey_ready, c + 1)
                    g.dma_start(ys_dram[ds(c * CH, CH), :], ey).then_inc(ys_out, 16)
                    g.wait_ge(ys_out, 16 * c + 16)
                    g.sem_inc(ey_room, 1)
            for i, (t0, n) in enumerate(TILES):
                g.indirect_dma_start(yg[0:n, i, :], None, ys_dram, bass.IndirectOffsetOnAxis(rowi[0:n, i:i + 1], 0))\
                    .then_inc(yg_in[i], 16)


def kernel(x, L0_tok_W, L0_attn_ln1_g, L0_attn_ln1_b, L0_attn_Wqkv, L0_attn_bqkv, L0_attn_Wo, L0_attn_bo,
           L0_attn_ln2_g, L0_attn_ln2_b, L0_attn_W1, L0_attn_b1, L0_attn_W2, L0_attn_b2, L0_ffn_W1, L0_ffn_b1,
           L0_ffn_W2, L0_ffn_b2, L0_ffn_Wr, L0_ffn_br):
    import concourse.bacc as bacc
    from concourse.bass_utils import run_bass_kernel_spmd

    def on_partitions(w):
        w = np.asarray(w)
        return w.reshape(-1, P, w.shape[-1]).transpose(1, 0, 2)

    heads = [t * 8 + half * 4 + h4 for half in range(2) for t in range(2) for h4 in range(4)]
    slot_cols = np.concatenate([np.arange(h * HD, (h + 1) * HD) for h in heads])
    qkv_cols = np.concatenate([np.arange(2 * D), 2 * D + slot_cols])

    patches = np.asarray(x).reshape(IMGS, 3, 6, 16, 6, 16).transpose(0, 1, 3, 5, 2, 4).reshape(TOK, 3 * 256).T
    w1e, w2e = np.asarray(L0_ffn_W1), np.asarray(L0_ffn_W2)
    experts = np.concatenate([w1e.reshape(E, KT, P, F).transpose(0, 2, 1, 3).reshape(E, P, KT * F),
                              w2e.reshape(E, FT, P, D).transpose(0, 2, 1, 3).reshape(E, P, FT * D)], axis=2)
    rows = np.concatenate([np.asarray(L0_attn_bqkv)[qkv_cols], np.asarray(L0_attn_bo), np.asarray(L0_attn_b2),
                           np.asarray(L0_ffn_br)])[None, :]
    cols = np.concatenate([np.asarray(a).reshape(-1, P).T for a in
                           (L0_attn_ln1_g, L0_attn_ln1_b, L0_attn_ln2_g, L0_attn_ln2_b, L0_attn_b1)], axis=1)
    arrays = {
        "xT": on_partitions(patches), "tokw": on_partitions(L0_tok_W),
        "wqkv": on_partitions(np.asarray(L0_attn_Wqkv)[:, qkv_cols]),
        "wo": on_partitions(np.asarray(L0_attn_Wo)[slot_cols]), "w1": on_partitions(L0_attn_W1),
        "w2": on_partitions(L0_attn_W2), "we": experts, "wr": on_partitions(L0_ffn_Wr), "rows": rows, "cols": cols,
        "eb": np.concatenate([np.asarray(L0_ffn_b1), np.asarray(L0_ffn_b2)], axis=1).reshape(P, -1), "consts": shape_constants(),
    }
    nc = bacc.Bacc("TRN2", target_bir_lowering=False, num_devices=1)
    arrays = {k: np.ascontiguousarray(a) for k, a in arrays.items()}
    args = [nc.dram_tensor(k + "_in", a.shape, F32, kind="ExternalInput").ap() for k, a in arrays.items()]
    out = nc.dram_tensor("out", (TOK, D), F32, kind="ExternalOutput").ap()
    tower(nc, *args, out)
    r = run_bass_kernel_spmd(nc, [{k + "_in": a for k, a in arrays.items()}], core_ids=[0])
    return r.results[0]["out"].reshape(IMGS, SEQ, D)
```

```python
from contextlib import ExitStack

import numpy as np
import concourse.bass as bass
from concourse.bass import ds
from concourse import mybir

ALU = mybir.AluOpType
ACT = mybir.ActivationFunctionType
F32 = mybir.dt.float32
BF16 = mybir.dt.bfloat16
I32 = mybir.dt.int32
AX = mybir.AxisListType.X

P = 128
IMGS, SEQ, D, H, HD = 16, 36, 256, 16, 16
TOK = IMGS * SEQ
KT = D // P
TILES = [(t, min(P, TOK - t)) for t in range(0, TOK, P)]
NT = len(TILES)
PATCH_K = 3 * 16 * 16 // P
F = 1024
FT = F // P
E = 8
PAIRS = IMGS // 2
EARLY_IMGS = 2 * P // SEQ // 2 * 2
HG = 3
GROUPS = [(o, min(HG, H - o)) for o in range(0, H, HG)]
VW = HD + 1
HB = 3 * HG
OT_AT = 2 * HB * VW
HO = 2 * HB
CH = P
NCH = (TOK - E) // CH + E
EXP_W = KT * F + FT * D
ROW_W = D + 2
EPS = 1e-5
NEG = -1e30


def const_layout():
    at, out = 0, {}
    for name, w in (("ident", P), ("headmask", 4), ("cos", NT * HD), ("sin", NT * HD), ("before", P), ("ones", P),
                    ("vmask", H * VW), ("causal", 8 * SEQ), ("id64", 64), ("valid", NT), ("tokno", NT), ("thr", E * NT),
                    ("upto", E * E), ("chunkno", (NCH + 1) * E), ("slotno", CH), ("eidx", E)):
        out[name] = (at, at + w)
        at += w
    return out, at


def shape_constants():
    lay, width = const_layout()
    c = np.zeros((P, width), np.float32)
    p = np.arange(P)

    def put(name, a):
        lo, hi = lay[name]
        c[:, lo:hi] = np.broadcast_to(a, (P,) + a.shape[1:]).reshape(P, hi - lo)

    put("ident", np.eye(P))
    put("headmask", ((p[:, None] % 64) // HD == np.arange(4)[None, :]).astype(np.float32))
    inv = 1.0 / 10000.0 ** (np.arange(0, HD, 2, dtype=np.float32) / np.float32(HD))
    pos = ((p[:, None] + P * np.arange(NT)[None, :]) % SEQ).astype(np.float32)
    ang = pos[:, :, None] * np.concatenate([inv, inv]).astype(np.float32)[None, None, :]
    sign = np.where(np.arange(HD) < HD // 2, -1.0, 1.0)
    put("cos", np.cos(ang))
    put("sin", np.sin(ang) * sign)
    put("before", (p[:, None] < p[None, :]).astype(np.float32))
    put("ones", np.ones((P, P)))
    vm = (p[:, None] // SEQ == np.arange(H)[None, :] % HG).astype(np.float32)
    put("vmask", np.repeat(vm, VW, axis=1))
    q = p % 64
    ca = np.where((q[:, None] < SEQ) & (np.arange(SEQ)[None, :] > q[:, None]), NEG, 0.0)
    put("causal", np.tile(ca, (1, 8)))
    put("id64", (q[:, None] == np.arange(64)[None, :]).astype(np.float32))
    put("valid", (p[:, None] + P * np.arange(NT)[None, :] < TOK).astype(np.float32))
    put("tokno", p[:, None] + P * np.arange(NT)[None, :] + 1.0)
    put("thr", np.tile(CH * np.arange(NT), E)[None, :])
    put("upto", (np.arange(E)[None, :] <= np.arange(E)[:, None]).astype(np.float32).reshape(1, -1))
    put("chunkno", np.repeat(np.arange(NCH + 1), E)[None, :])
    put("slotno", np.arange(CH)[None, :])
    put("eidx", np.arange(E)[None, :])
    return c


def tower(nc, xT_d, tokw_d, wqkv_d, wo_d, w1_d, w2_d, we_d, wr_d, b1_d, rows_d, cols_d, eb_d, const_d, out_d):
    ctx = ExitStack()
    with ctx:
        def sb(name, shape, dt=F32):
            return ctx.enter_context(nc.sbuf_tensor(name, shape, dt))

        def sem(name):
            return ctx.enter_context(nc.semaphore(name))

        lay, cw = const_layout()
        const = sb("const", [P, cw])

        def cst(name):
            return const[:, lay[name][0]:lay[name][1]]

        ident = cst("ident")
        xs_dram = nc.dram_tensor("chunk_rows", [(NCH + 1) * CH, ROW_W], F32, kind="Internal").ap()
        eb_dram = nc.dram_tensor("expert_bias_parts", [3, E * D], BF16, kind="Internal").ap()
        v_dram = nc.dram_tensor("v_scratch", [TOK, D], F32, kind="Internal").ap()

        RES = 3
        we = sb("expert_w", [P, E * EXP_W])
        early = we[:, RES * EXP_W:E * EXP_W]
        at = [0]

        def carve(n):
            at[0] += n
            assert at[0] <= (E - RES) * EXP_W
            return early[:, at[0] - n:at[0]]

        vb = carve(IMGS * HO * VW).rearrange("p (i o c) -> p i o c", i=IMGS, o=HO)
        vrep = carve(IMGS * D).rearrange("p (i c) -> p i c", i=IMGS)
        tokw = carve(PATCH_K * D).rearrange("p (k n) -> p k n", k=PATCH_K)
        wqkv = carve(KT * 3 * D).rearrange("p (k n) -> p k n", k=KT)
        at[0] = 3 * EXP_W
        km_f = carve(KT * 4 * TOK)
        km = km_f.rearrange("p (t h n) -> p t h n", t=KT, h=4)
        xT = km_f[:, 0:PATCH_K * TOK].rearrange("p (k n) -> p k n", k=PATCH_K)
        hidT = km_f[:, 0:FT * TOK].rearrange("p (k n) -> p k n", k=FT)
        wo = sb("wo", [P, KT, D])
        w1 = carve(KT * F).rearrange("p (k n) -> p k n", k=KT)
        w2 = sb("w2", [P, FT, D])
        wr = sb("wr", [P, KT, E])
        b1 = sb("b1", [P, E * FT])
        b1s = sb("b1s", [P, FT])
        rows = sb("rows", [P, 5 * D + E])
        cols = sb("cols", [P, 4 * KT + FT])
        res = sb("res", [P, NT, D])
        mid = sb("mid", [P, NT, D])
        pay = sb("pay", [P, NT, ROW_W])
        x2 = carve(NT * D).rearrange("p (i c) -> p i c", i=NT)
        nT = sb("nT", [P, KT, TOK])
        oT = nT
        bst = sb("bst", [P, NT, 6])
        mv = sb("mv", [P, NT, 2])
        nw = sb("nw", [P, 4, NT])
        scr = sb("scr", [P, 6336 + 2 * HO * HD])
        nrm = [x2, scr[:, 0:NT * D].rearrange("p (i c) -> p i c", i=NT), pay]
        qk = scr[:, 0:1024].rearrange("p (b n) -> p b n", b=2)
        ropec = scr[:, 1024:2048].rearrange("p (b n) -> p b n", b=2)
        ropes = scr[:, 2048:3072].rearrange("p (b n) -> p b n", b=2)
        vt = mid
        QTW = TOK + 32
        qT = scr[:, 3584:3584 + KT * QTW].rearrange("p (t n) -> p t n", t=KT)
        dif = scr[:, 0:1152].rearrange("p (b n) -> p b n", b=2)
        prob = scr[:, 1152:2304].rearrange("p (b n) -> p b n", b=2)
        pT = scr[:, 4800:4800 + 1536].rearrange("p (b g n) -> p b g n", b=2, g=len(GROUPS))
        on = scr[:, 6336:6336 + 2 * HO * HD].rearrange("p (b n) -> p b n", b=2)
        xe = scr[:, 0:ROW_W]
        xeT = scr[:, ROW_W:ROW_W + D].rearrange("p (k n) -> p k n", k=KT)
        gh = scr[:, 3072:3072 + F].rearrange("p (k n) -> p k n", k=FT)
        eh = scr[:, 3072 + F:3072 + 2 * F].rearrange("p (k n) -> p k n", k=FT)
        w1s = w2
        perm = nT[:, :, :].rearrange("p k n -> p (k n)")[:, 0:NT * CH].rearrange("p (i n) -> p i n", i=NT)
        ez = res[:, 0, :]
        eout = res[:, 1, :]
        xk = mid[:, :, :].rearrange("p i c -> p (i c)")
        ebr = scr[0:3, NT * D:NT * D + E * D // 2].bitcast(BF16)
        zero = pay[:, 0, :]
        est = sb("est", [P, 16])
        eti = sb("eti", [P, 1], I32)
        EBP = E * D // P
        ebf = sb("ebf", [P, 3, EBP])
        ebp = sb("ebp", [P, 3, EBP], BF16)
        lg = sb("lg", [P, NT, E])
        lmax = sb("lmax", [P, NT])
        first = sb("first", [P, NT, E])
        gate = sb("gate", [P, NT])
        onehot = sb("onehot", [P, NT, E])
        onehotb = sb("onehotb", [P, NT, E], BF16)
        beforeb = sb("beforeb", [P, P], BF16)
        onesb = sb("onesb", [P, P], BF16)
        cnt = sb("cnt", [P, 4, E])
        tmp = sb("tmp", [P, (NCH + 1) * E])
        meta = sb("meta", [P, NCH + 1])
        metai = sb("metai", [P, NCH + 2], I32)
        row = sb("row", [P, NT])
        rowi = sb("rowi", [P, NT], I32)
        mx = sb("mx", [P, 2, H])
        rinv = sb("rinv", [P, 2, HO])
        caus = sb("caus", [P, 8 * SEQ], BF16)
        id64 = sb("id64b", [P, 64], BF16)

        bank = [ctx.enter_context(nc.psum_tensor(f"bank{b}", [P, 512], F32)) for b in range(4)]
        bank45 = ctx.enter_context(nc.psum_tensor("bank45", [P, 1024], F32))
        bank += [bank45[:, 0:512], bank45[:, 512:1024]]
        bank67 = ctx.enter_context(nc.psum_tensor("bank67", [P, 1024], F32))
        bank += [bank67[:, 0:512], bank67[:, 512:1024]]

        xt_in = [sem(f"xt_in{k}") for k in range(PATCH_K)]
        const_in = sem("const_in")
        rows_in = sem("rows_in")
        wqkv_in = sem("wqkv_in")
        mlp_in = sem("mlp_in")
        vt_out = [sem(f"vt_out{i}") for i in range(NT)]
        vrep_in = [sem(f"vrep_in{s}") for s in range(2)]
        out_st = sem("out_st")
        tok_mm = sem("tok_mm")
        res_ready = sem("res_ready")
        dve = sem("dve")
        pl = sem("pl")
        nrm_ready = [sem(f"nrm_ready{l}") for l in range(3)]
        nT_mm = [sem(f"nT_mm{l}") for l in range(3)]
        nT_ready = [sem(f"nT_ready{l}") for l in range(3)]
        qk_mm = sem("qk_mm")
        v_mm = sem("v_mm")
        qk_ready = sem("qk_ready")
        ropec_ready = sem("ropec_ready")
        ropes_ready = sem("ropes_ready")
        rope_ready = sem("rope_ready")
        vt_ready = sem("vt_ready")
        qkT_mm = sem("qkT_mm")
        qT_ready = sem("qT_ready")
        km_ready = sem("km_ready")
        qpad_ready = sem("qpad_ready")
        mask_ready = sem("mask_ready")
        vb_ready = sem("vb_ready")
        score_mm = sem("score_mm")
        dif_ready = sem("dif_ready")
        prob_ready = sem("prob_ready")
        pT_mm = sem("pT_mm")
        pT_ready = sem("pT_ready")
        av_mm = sem("av_mm")
        on_ready = sem("on_ready")
        oT_mm = sem("oT_mm")
        oT_ready = sem("oT_ready")
        mid_ready = sem("mid_ready")
        wo_mm = sem("wo_mm")
        x2_ready = sem("x2_ready")
        hx_ready = sem("hx_ready")
        up_mm = sem("up_mm")
        hid_ready = sem("hid_ready")
        down_mm = sem("down_mm")
        x3_ready = sem("x3_ready")
        we_in = [sem(f"we_in{e}") for e in range(E)]
        b1_in = sem("b1_in")
        eb_in = sem("eb_in")
        eb_split = sem("eb_split")
        eb_rest = sem("eb_rest")
        ebp_out = sem("ebp_out")
        ebr_in = sem("ebr_in")
        zero_ready = sem("zero_ready")
        rows_cleared = sem("rows_cleared")
        bf_ready = sem("bf_ready")
        logit_mm = sem("logit_mm")
        shift_ready = sem("shift_ready")
        expl_ready = sem("expl_ready")
        onehot_ready = sem("onehot_ready")
        rank_mm = sem("rank_mm")
        stat_ready = sem("stat_ready")
        row_ready = sem("row_ready")
        pay_ready = sem("pay_ready")
        meta_ready = sem("meta_ready")
        xs_out = sem("xs_out")
        xe_in = sem("xe_in")
        xeT_mm = sem("xeT_mm")
        xeT_ready = sem("xeT_ready")
        perm_ready = sem("perm_ready")
        b1s_ready = sem("b1s_ready")
        w1s_ready, eup_mm, gh_ready, eh_ready = ([sem(f"{name}{s}") for s in range(2)] for name in
                                                 ("w1s_ready", "eup_mm", "gh_ready", "eh_ready"))
        ey_mm = sem("ey_mm")
        xk_ready = sem("xk_ready")
        y_room = sem("y_room")
        eout_ready = sem("eout_ready")
        store_begun = sem("store_begun")
        eout_room = sem("eout_room")
        estep = [sem(f"estep{j}") for j in range(14)]

        block = ctx.enter_context(nc.Block())

        def inverse_root(eng, link, vh, y, a, b, var):
            link(eng.tensor_scalar(vh, var, EPS, -0.5, ALU.add, ALU.mult))
            link(eng.tensor_scalar(y.bitcast(I32), vh.bitcast(I32), -0.5, float(0x5F3759DF - 0x40400000),
                                   ALU.mult, ALU.add))
            for _ in range(3):
                if y.shape[1] == 1:
                    link(eng.scalar_tensor_tensor(out=b, in0=y, scalar=y, in1=vh, op0=ALU.mult, op1=ALU.mult))
                else:
                    link(eng.tensor_tensor(a, y, y, ALU.mult))
                    link(eng.tensor_tensor(b, a, vh, ALU.mult))
                link(eng.scalar_tensor_tensor(out=y, in0=b, scalar=1.5, in1=y, op0=ALU.add, op1=ALU.mult))

        def chunks_in_use(eng):
            eng.wait_ge(meta_ready, 2)
            return eng.value_load(metai[0:1, NCH + 1:NCH + 2], min_val=1, max_val=NCH)

        @block.sync
        def _(sp):
            for k in range(PATCH_K):
                sp.dma_start(xT[:, k, :], xT_d[:, k, :]).then_inc(xt_in[k], 16)
                sp.dma_start(tokw[:, k, :], tokw_d[:, k, :]).then_inc(xt_in[k], 16)
            sp.dma_start(const[:, :], const_d).then_inc(const_in, 16)
            sp.dma_start(cols[:, :], cols_d).then_inc(const_in, 16)
            sp.dma_start(rows[:, :], rows_d.broadcast_to((P, 5 * D + E))).then_inc(rows_in, 16)
            sp.dma_start(wqkv[:, :, :], wqkv_d).then_inc(wqkv_in, 16)
            sp.dma_start(wo[:, :, :], wo_d).then_inc(mlp_in, 16)
            sp.dma_start(w1[:, :, :], w1_d).then_inc(mlp_in, 16)
            sp.dma_start(w2[:, :, :], w2_d).then_inc(mlp_in, 16)
            sp.dma_start(wr[:, :, :], wr_d).then_inc(mlp_in, 16)
            sp.dma_start(b1[:, :], b1_d).then_inc(b1_in, 16)
            sp.dma_start(ebf[:, 0, :], eb_d).then_inc(eb_in, 16)
            sp.wait_ge(zero_ready, 1)
            sp.dma_start(xs_dram.rearrange("(c p) d -> p c d", p=CH),
                         zero.rearrange("p (o d) -> p o d", o=1).broadcast_to((P, NCH + 1, ROW_W)))\
                .then_inc(rows_cleared, 16)
            for i, (t0, n) in enumerate(TILES):
                sp.wait_ge(vt_ready, i + 1)
                sp.dma_start(v_dram[t0:t0 + n, :], vt[0:n, i, :]).then_inc(vt_out[i], 16)
                if i in (2, NT - 1):
                    part = 0 if i == 2 else 1
                    lo, hi = (0, EARLY_IMGS) if part == 0 else (EARLY_IMGS, IMGS)
                    for t in range(2) if part == 0 else range(2, NT):
                        sp.wait_ge(vt_out[t], 16)
                    for j in range(HG):
                        sp.dma_start(vrep[SEQ * j:SEQ * (j + 1), lo:hi, :],
                                     v_dram.rearrange("(i k) c -> k i c", k=SEQ)[:, lo:hi, :])\
                            .then_inc(vrep_in[part], 16)
            for e in range(RES):
                sp.dma_start(we[:, e * EXP_W:(e + 1) * EXP_W], we_d[e]).then_inc(we_in[e], 16)
            sp.wait_ge(eb_split, 3)
            sp.dma_start(eb_dram.rearrange("s (p c) -> p s c", p=P), ebp[:, :, :]).then_inc(ebp_out, 16)
            sp.wait_ge(av_mm, PAIRS)
            sp.wait_ge(ebp_out, 16)
            for e in range(RES, 6):
                sp.dma_start(we[:, e * EXP_W:(e + 1) * EXP_W], we_d[e]).then_inc(we_in[e], 16)
            sp.wait_ge(oT_ready, PAIRS)
            sp.dma_start(ebr, eb_dram).then_inc(ebr_in, 16)
            sp.wait_ge(down_mm, NT)
            sp.wait_ge(hx_ready, NT)
            for e in range(6, E):
                sp.dma_start(we[:, e * EXP_W:(e + 1) * EXP_W], we_d[e]).then_inc(we_in[e], 16)
            n_chunks = chunks_in_use(sp)
            sp.wait_ge(xs_out, 16 * NT)
            sp.dma_start(xe, xs_dram[0:CH, :]).then_inc(xe_in, 16)
            with sp.Fori(1, NCH + 1) as c:
                with sp.If(c < n_chunks + 1):
                    sp.wait_ge(xeT_mm, c)
                    sp.wait_ge(xk_ready, c)
                    sp.dma_start(xe, xs_dram[ds(c * CH, CH), :]).then_inc(xe_in, 16)

        @block.tensor
        def _(pe):
            def transpose_tile(l, i):
                t0, n = TILES[i]
                b = bank[(1 if l == 2 else 5) + i % 2]
                pe.wait_ge(nrm_ready[l], i + 1)
                if i >= 2:
                    pe.wait_ge(nT_ready[l], i - 1)
                for k in range(KT):
                    last = pe.transpose(b[:, k * P:k * P + n], nrm[l][0:n, i, k * P:(k + 1) * P], ident[0:n, 0:n])
                last.then_inc(nT_mm[l], 1)

            for k in range(PATCH_K):
                pe.wait_ge(xt_in[k], 32)
                for i, (t0, n) in enumerate(TILES):
                    last = pe.matmul(bank[i][0:n, 0:D], xT[:, k, t0:t0 + n], tokw[:, k, :],
                                     start=(k == 0), stop=(k == PATCH_K - 1))
                    if k == PATCH_K - 1:
                        last.then_inc(tok_mm, 1)
            pe.wait_ge(const_in, 32)

            def project(i):
                t0, n = TILES[i]
                pe.wait_ge(nT_ready[0], i + 1)
                if i == 0:
                    pe.wait_ge(wqkv_in, 16)
                if i < 2:
                    pe.wait_ge(res_ready, 2 * i + 2)
                if i >= 2:
                    pe.wait_ge(qk_ready, i - 1)
                    pe.wait_ge(vt_ready, i - 1)
                for k in range(KT):
                    last = pe.matmul(bank[2 * (i % 2)][0:n, :], nT[:, k, t0:t0 + n], wqkv[:, k, 0:2 * D],
                                     start=(k == 0), stop=(k == KT - 1))
                last.then_inc(qk_mm, 1)
                for k in range(KT):
                    last = pe.matmul(bank[2 * (i % 2) + 1][0:n, 0:D], nT[:, k, t0:t0 + n], wqkv[:, k, 2 * D:3 * D],
                                     start=(k == 0), stop=(k == KT - 1))
                last.then_inc(v_mm, 1)

            def turn_qk(i):
                t0, n = TILES[i]
                pe.wait_ge(rope_ready, i + 1)
                if i == 0:
                    pe.wait_ge(res_ready, NT)
                else:
                    pe.wait_ge(qT_ready, i)
                    pe.wait_ge(km_ready, i)
                for j, dst in enumerate((bank[4][:, 0:P], bank[4][:, P:2 * P], bank[7][:, 0:P], bank[4][:, 2 * P:3 * P])):
                    last = pe.transpose(dst[:, 0:n], ropec[0:n, i % 2, j * P:(j + 1) * P], ident[0:n, 0:n])
                last.then_inc(qkT_mm, 1)

            transpose_tile(0, 0)
            transpose_tile(0, 1)
            for i in range(NT):
                project(i)
                if i + 2 < NT:
                    transpose_tile(0, i + 2)
                if i >= 1:
                    turn_qk(i - 1)
            turn_qk(NT - 1)

            def scores(p):
                if p == 0:
                    pe.wait_ge(qT_ready, NT)
                    pe.wait_ge(km_ready, NT)
                    pe.wait_ge(qpad_ready, 1)
                    pe.wait_ge(mask_ready, 2)
                    pe.wait_ge(vt_ready, NT)
                if p >= 2:
                    pe.wait_ge(dif_ready, p - 1)
                for half in range(2):
                    s = [bank[2 * (p % 2) + half][64 * im:64 * im + 64, :] for im in range(2)]
                    r = slice(64 * half, 64 * half + 64)
                    for im in range(2):
                        pe.matmul(s[im][:, 0:8 * SEQ], id64[r, :], caus[r, :], start=True, stop=False,
                                  skip_group_check=True)
                    for t in range(KT):
                        for im in range(2):
                            q0 = (2 * p + im) * SEQ
                            last = pe.matmul(s[im][:, t * 4 * SEQ:(t + 1) * 4 * SEQ], qT[r, t, q0:q0 + 64],
                                             km[r, t, :, q0:q0 + SEQ], start=False, stop=True, skip_group_check=True)
                last.then_inc(score_mm, 1)

            def turn_probs(p):
                pe.wait_ge(prob_ready, p + 1)
                if p >= 1:
                    pe.wait_ge(pT_ready, p)
                else:
                    pe.wait_ge(nT_ready[0], NT)
                for g, (o, nh) in enumerate(GROUPS):
                    last = pe.transpose(bank45[0:nh * SEQ, g * P:(g + 1) * P],
                                        prob[:, p % 2, o * SEQ:(o + nh) * SEQ], ident)
                last.then_inc(pT_mm, 1)

            def values(p):
                pe.wait_ge(pT_ready, p + 1)
                pe.wait_ge(vb_ready, p + 2)
                if p >= 1:
                    pe.wait_ge(on_ready, p)
                    pe.wait_ge(oT_ready, p)
                for g, (o, nh) in enumerate(GROUPS):
                    dst = bank[6 + g // 3][:, 0:2 * HB * VW].rearrange("p (i n) -> p i n", i=2)
                    last = pe.matmul(dst[:, :, (g % 3) * HG * VW:(g % 3 + 1) * HG * VW], pT[0:nh * SEQ, p % 2, g, :],
                                     vb[0:nh * SEQ, 2 * p:2 * p + 2, o:o + HG, :].rearrange("p i o c -> p i (o c)"),
                                     start=True, stop=True)
                last.then_inc(av_mm, 1)

            def turn_out(p):
                pe.wait_ge(on_ready, p + 1)
                for k in range(KT):
                    last = pe.transpose(bank[6 + k][:, OT_AT:OT_AT + P], on[:, p % 2, k * P:(k + 1) * P], ident)
                last.then_inc(oT_mm, 1)

            def out_proj(i):
                t0, n = TILES[i]
                if i == 0:
                    pe.wait_ge(mlp_in, 64)
                    pe.wait_ge(dif_ready, PAIRS)
                if i == 4:
                    pe.wait_ge(pT_ready, PAIRS)
                pe.wait_ge(oT_ready, -(-(t0 + n) // (2 * SEQ)))
                for k in range(KT):
                    last = pe.matmul(bank[i][0:n, 0:D], oT[:, k, t0:t0 + n], wo[:, k, :],
                                     start=(k == 0), stop=(k == KT - 1))
                last.then_inc(wo_mm, 1)

            for p in range(PAIRS + 3):
                if p < PAIRS:
                    scores(p)
                if 3 <= p:
                    turn_out(p - 3)
                if 1 <= p <= PAIRS:
                    turn_probs(p - 1)
                if 2 <= p <= PAIRS + 1:
                    values(p - 2)
                if p == PAIRS:
                    for i in range(3):
                        out_proj(i)
            for i in range(3, NT):
                out_proj(i)
            HT = TOK // 2
            half_tiles = [-(-HT * (s + 1) // P) for s in range(2)]
            for s in range(2):
                if s == 0:
                    for i in range(half_tiles[0]):
                        transpose_tile(1, i)
                pe.wait_ge(nT_ready[1], half_tiles[s])
                for j in range(FT):
                    q = s * FT + j
                    if q == 0:
                        pe.wait_ge(x2_ready, NT)
                    if q == FT - 3:
                        for i in range(half_tiles[0], NT):
                            transpose_tile(1, i)
                    if q >= 4:
                        pe.wait_ge(hid_ready, q - 3)
                    for k in range(KT):
                        last = pe.matmul(bank[q % 4][:, 0:HT], w1[:, k, j * P:(j + 1) * P],
                                         nT[:, k, s * HT:(s + 1) * HT], start=(k == 0), stop=(k == KT - 1))
                    last.then_inc(up_mm, 1)
            for i, (t0, n) in enumerate(TILES):
                pe.wait_ge(hid_ready, FT if t0 + n <= HT else 2 * FT)
                if i == 1:
                    pe.wait_ge(nT_ready[1], NT)
                for j in range(FT):
                    last = pe.matmul(bank[(4 + i) % 8][0:n, 0:D], hidT[:, j, t0:t0 + n], w2[:, j, :],
                                     start=(j == 0), stop=(j == FT - 1))
                last.then_inc(down_mm, 1)

            def logits(i):
                t0, n = TILES[i]
                pe.wait_ge(nT_ready[2], i + 1)
                for k in range(KT):
                    last = pe.matmul(bank[3][0:n, i * E:(i + 1) * E], nT[:, k, t0:t0 + n], wr[:, k, :],
                                     start=(k == 0), stop=(k == KT - 1))
                return last

            transpose_tile(2, 0)
            for i in range(1, NT):
                transpose_tile(2, i)
                logits(i - 1)
            last = logits(NT - 1)
            last.then_inc(logit_mm, 1)
            pe.wait_ge(onehot_ready, 1)
            pe.wait_ge(bf_ready, 2)
            for i in range(NT + 1):
                for j in range(min(i + 1, NT)):
                    last = pe.matmul(bank[4][:, i * E:(i + 1) * E], beforeb[:, :] if j == i else onesb[:, :],
                                     onehotb[:, j, :], start=(j == 0), stop=(j == min(i, NT - 1)))
            last.then_inc(rank_mm, 1)

            def turn_rows(c):
                pe.wait_ge(xe_in, 16 * (c + 1))
                for k in range(KT):
                    last = pe.transpose(bank[5][:, k * P:(k + 1) * P], xe[:, k * P:(k + 1) * P], ident)
                last.then_inc(xeT_mm, 1)

            def expert_up(c, first):
                pe.wait_ge(xeT_ready, c + 1)
                for s in range(2):
                    pe.wait_ge(w1s_ready[s], c + 1)
                    if not first:
                        pe.wait_ge(gh_ready[s], c)
                    for j in range(4):
                        for k in range(KT):
                            at = (2 * s + k) * 512 + j * P
                            last = pe.matmul(bank[s][:, j * P:(j + 1) * P], w1s[:, at // D, at % D:at % D + P],
                                             xeT[:, k, :], start=(k == 0), stop=(k == KT - 1))
                    last.then_inc(eup_mm[s], 1)

            def expert_down(done, e):
                pe.wait_ge(eh_ready[0], done)
                pe.wait_ge(y_room, done)
                pe.matmul(bank[6][:, 0:D], onesb[0:3, :], ebr[:, ds(e * D, D)], start=True, stop=False)
                for j in range(FT):
                    if j == 4:
                        pe.wait_ge(eh_ready[1], done)
                    last = pe.matmul(bank[6][:, 0:D], eh[:, j, :], we[:, ds(e * EXP_W + KT * F + j * D, D)],
                                     start=False, stop=(j == FT - 1))
                last.then_inc(ey_mm, 1)

            pe.wait_ge(perm_ready, 1)
            pe.wait_ge(shift_ready, 1)
            for k in range(KT):
                for i, (t0, n) in enumerate(TILES):
                    last = pe.matmul(bank[5][:, k * P:(k + 1) * P], pay[0:n, i, k * P:(k + 1) * P], perm[0:n, i, :],
                                     start=(i == 0), stop=(i == NT - 1))
            last.then_inc(xeT_mm, 1)
            n_chunks = chunks_in_use(pe)

            def expert_of(c):
                return pe.value_load(metai[0:1, ds(c, 1)], min_val=0, max_val=E - 1)

            pe.wait_ge(ebr_in, 16)
            for e in range(E):
                pe.wait_ge(we_in[e], 16)
            expert_up(0, True)
            turn_rows(1)
            expert_up(1, False)
            turn_rows(2)
            expert_down(1, expert_of(0))
            with pe.Fori(2, NCH) as c:
                with pe.If(c < n_chunks):
                    expert_up(c, False)
                    turn_rows(c + 1)
                    expert_down(c, expert_of(c - 1))
            expert_down(n_chunks, expert_of(n_chunks - 1))

        @block.vector
        def _(v):
            count = [0]

            def link(ins):
                count[0] += 1
                ins.then_inc(dve, 1)
                v.wait_ge(dve, count[0])

            def stats(src, i):
                n = TILES[i][1]
                link(v.bn_stats(bst[0:n, i, :], src[0:n, i, :]))
                v.bn_aggr(mv[0:n, i, :], bst[0:n, i, :]).then_inc(stat_ready, 1)

            seen = [0]

            def normalise(l, src, lo, hi):
                seen[0] += hi - lo
                v.wait_ge(stat_ready, seen[0])
                vh, y, a, b = (nw[:, j, lo:hi] for j in range(4))
                inverse_root(v, link, vh, y, a, b, mv[:, lo:hi, 1])
                for i in range(lo, hi):
                    n = TILES[i][1]
                    v.tensor_scalar(nrm[l][0:n, i, 0:D], src[0:n, i, :], mv[0:n, i, 0:1], nw[0:n, 1, i:i + 1],
                                    ALU.subtract, ALU.mult).then_inc(nrm_ready[l], 1)

            def empty_qkv(i):
                t0, n = TILES[i]
                v.wait_ge(qk_mm, i + 1)
                if i == 0:
                    v.wait_ge(rows_in, 16)
                if i >= 2:
                    v.wait_ge(ropec_ready, i - 1)
                v.tensor_tensor(qk[0:n, i % 2, :], bank[2 * (i % 2)][0:n, :], rows[0:n, 0:2 * D],
                                ALU.add).then_inc(qk_ready, 1)
                v.wait_ge(v_mm, i + 1)
                v.tensor_tensor(vt[0:n, i, :], bank[2 * (i % 2) + 1][0:n, 0:D], rows[0:n, 2 * D:3 * D],
                                ALU.add).then_inc(vt_ready, 1)
                v.wait_ge(qk_ready, i + 1)
                if i >= 2:
                    v.wait_ge(rope_ready, i - 1)
                q4 = qk[0:n, i % 2, :].rearrange("p (h a c) -> p h a c", a=2, c=HD // 2)
                s4 = ropes[0:n, i % 2, :].rearrange("p (h a c) -> p h a c", a=2, c=HD // 2)
                sn = cst("sin")[0:n, i * HD:(i + 1) * HD].rearrange("p (o a c) -> p o a c", o=1, a=2)
                for a in range(2):
                    last = v.tensor_tensor(s4[:, :, a, :], q4[:, :, 1 - a, :],
                                           sn[:, :, a, :].broadcast_to((n, 2 * H, HD // 2)), ALU.mult)
                last.then_inc(ropes_ready, 1)

            def mask_keys(i):
                t0, n = TILES[i]
                v.wait_ge(qkT_mm, i + 1)
                src = bank[7][:, 0:n].rearrange("p (o n) -> p o n", o=1).broadcast_to((P, 4, n))
                hm = cst("headmask").rearrange("p (h o) -> p h o", o=1).broadcast_to((P, 4, n))
                v.tensor_tensor(km[:, 0, :, t0:t0 + n], src, hm, ALU.mult).then_inc(km_ready, 1)

            link(v.memset(mv[:, :, :], 1.0))
            link(v.memset(lg[:, :, :], 0.0))
            for lo, hi in ((0, 2), (2, NT)):
                for i in range(lo, hi):
                    v.wait_ge(res_ready, i + 1)
                    stats(res, i)
                normalise(0, res, lo, hi)
            v.wait_ge(const_in, 32)
            for i in range(NT):
                empty_qkv(i)
                if i >= 1:
                    mask_keys(i - 1)
            mask_keys(NT - 1)

            def soft_in(p):
                v.wait_ge(score_mm, p + 1)
                if p == 0:
                    v.wait_ge(qkT_mm, NT)
                    v.wait_ge(ropec_ready, NT)
                if p >= 2:
                    v.wait_ge(prob_ready, p - 1)
                for half in range(2):
                    s = bank[2 * (p % 2) + half][:, 0:8 * SEQ].rearrange("p (h k) -> p h k", k=SEQ)
                    link(v.tensor_reduce(mx[:, p % 2, 8 * half:8 * half + 8], s, AX, ALU.max))
                for half in range(2):
                    s = bank[2 * (p % 2) + half][:, 0:8 * SEQ].rearrange("p (h k) -> p h k", k=SEQ)
                    m = mx[:, p % 2, 8 * half:8 * half + 8].rearrange("p (h o) -> p h o", o=1).broadcast_to((P, 8, SEQ))
                    d = dif[:, p % 2, half * 8 * SEQ:(half + 1) * 8 * SEQ].rearrange("p (h k) -> p h k", k=SEQ)
                    last = v.tensor_tensor(d, s, m, ALU.subtract)
                last.then_inc(dif_ready, 1)

            def soft_out(p):
                v.wait_ge(av_mm, p + 1)
                if p >= 2:
                    v.wait_ge(oT_mm, p - 1)
                o4 = bank67[:, :].rearrange("p (b n) -> p b n", b=2)[:, :, 0:2 * HB * VW]\
                    .rearrange("p b (i o c) -> p b i o c", i=2, c=VW)
                for im in range(2):
                    r = slice(64 * im, 64 * im + 64)
                    last = v.reciprocal(rinv[r, p % 2, :].rearrange("p (b h) -> p b h", b=2), o4[r, :, im, :, HD])
                link(last)
                for im in range(2):
                    r = slice(64 * im, 64 * im + 64)
                    for b in range(2):
                        last = v.tensor_tensor(
                            on[r, p % 2, b * HB * HD:(b + 1) * HB * HD].rearrange("p (o c) -> p o c", c=HD),
                            o4[r, b, im, :, 0:HD],
                            rinv[r, p % 2, b * HB:(b + 1) * HB].rearrange("p (h o) -> p h o", o=1)
                            .broadcast_to((64, HB, HD)), ALU.mult)
                last.then_inc(on_ready, 1)

            for p in range(PAIRS + 2):
                if p < PAIRS:
                    soft_in(p)
                if p >= 2:
                    soft_out(p - 2)

            for lo, hi in ((0, 3), (3, NT)):
                for i in range(lo, hi):
                    n = TILES[i][1]
                    v.wait_ge(wo_mm, i + 1)
                    v.wait_ge(mid_ready, i + 1)
                    v.tensor_tensor(x2[0:n, i, :], bank[i][0:n, 0:D], mid[0:n, i, :], ALU.add).then_inc(x2_ready, 1)
                    v.wait_ge(x2_ready, i + 1)
                    stats(x2, i)
                normalise(1, x2, lo, hi)

            v.wait_ge(rows_cleared, 16)
            for lo, hi in ((0, NT - 2), (NT - 2, NT - 1), (NT - 1, NT)):
                for i in range(lo, hi):
                    n = TILES[i][1]
                    v.wait_ge(down_mm, i + 1)
                    v.wait_ge(hx_ready, i + 1)
                    link(v.tensor_tensor(mid[0:n, i, :], bank[(4 + i) % 8][0:n, 0:D], res[0:n, i, :], ALU.add))
                    stats(mid, i)
                normalise(2, mid, lo, hi)

            lgb = [P, NT, E]
            v.tensor_copy(pay[:, :, D + 1], cst("tokno")).then_inc(pay_ready, 1)
            v.wait_ge(logit_mm, 1)
            full = NT - 1
            last_n = TILES[full][1]
            br = rows[:, 5 * D:5 * D + E].rearrange("p (o e) -> p o e", o=1)
            link(v.tensor_tensor(lg[:, 0:full, :], bank[3][:, 0:full * E].rearrange("p (i e) -> p i e", e=E),
                                 br.broadcast_to((P, full, E)), ALU.add))
            link(v.tensor_tensor(lg[0:last_n, full, :], bank[3][0:last_n, full * E:NT * E], rows[0:last_n, 5 * D:],
                                 ALU.add))
            link(v.tensor_reduce(lmax[:, :], lg[:, :, :], AX, ALU.max))
            top = lmax[:, :].rearrange("p (i o) -> p i o", o=1).broadcast_to(lgb)
            link(v.tensor_tensor(first[:, :, :], lg[:, :, :], top, ALU.is_equal))
            v.tensor_tensor(lg[:, :, :], lg[:, :, :], top, ALU.subtract).then_inc(shift_ready, 1)
            eidx = cst("eidx").rearrange("p (o e) -> p o e", o=1).broadcast_to(lgb)
            link(v.scalar_tensor_tensor(out=first[:, :, :], in0=first[:, :, :], scalar=-float(E), in1=eidx,
                                        op0=ALU.mult, op1=ALU.add))
            link(v.tensor_reduce(row[:, :], first[:, :, :], AX, ALU.min))
            link(v.tensor_tensor(onehot[:, :, :], first[:, :, :],
                                 row[:, :].rearrange("p (i o) -> p i o", o=1).broadcast_to(lgb), ALU.is_equal))
            valid = cst("valid").rearrange("p (i o) -> p i o", o=1).broadcast_to(lgb)
            v.tensor_tensor(onehotb[:, :, :], onehot[:, :, :], valid, ALU.mult).then_inc(onehot_ready, 1)
            v.wait_ge(expl_ready, 1)
            link(v.tensor_reduce(gate[:, :], lg[:, :, :], AX, ALU.add))
            v.reciprocal(pay[:, :, D], gate[:, :]).then_inc(pay_ready, 1)

            v.wait_ge(rank_mm, 1)
            v.wait_ge(onehot_ready, 1)
            ranks = bank[4][:, 0:NT * E].rearrange("p (i e) -> p i e", e=E)
            link(v.tensor_copy(cnt[:, 0, :], bank[4][:, NT * E:(NT + 1) * E]))
            t5 = tmp[:, 0:E * NT].rearrange("p (e j) -> p e j", e=E)
            link(v.tensor_tensor(t5, cnt[:, 0, :].rearrange("p (e o) -> p e o", o=1).broadcast_to((P, E, NT)),
                                 cst("thr").rearrange("p (e j) -> p e j", e=E), ALU.is_gt))
            link(v.tensor_reduce(cnt[:, 1, :], t5, AX, ALU.add))
            t8 = tmp[:, 0:E * E].rearrange("p (a b) -> p a b", a=E)
            link(v.tensor_tensor(t8, cnt[:, 1, :].rearrange("p (o e) -> p o e", o=1).broadcast_to((P, E, E)),
                                 cst("upto").rearrange("p (a b) -> p a b", a=E), ALU.mult))
            link(v.tensor_reduce(cnt[:, 2, :], t8, AX, ALU.add))
            link(v.tensor_tensor(cnt[:, 3, :], cnt[:, 2, :], cnt[:, 1, :], ALU.subtract))
            link(v.scalar_tensor_tensor(out=first[:, :, :],
                                        in0=cnt[:, 3, :].rearrange("p (o e) -> p o e", o=1).broadcast_to(lgb),
                                        scalar=float(CH), in1=ranks, op0=ALU.mult, op1=ALU.add))
            link(v.tensor_tensor(first[:, :, :], first[:, :, :], onehot[:, :, :], ALU.mult))
            link(v.tensor_reduce(row[:, :], first[:, :, :], AX, ALU.add))
            v.tensor_copy(rowi[:, :], row[:, :]).then_inc(row_ready, 1)
            v.wait_ge(logit_mm, 1)
            v.tensor_tensor(perm, row[:, :].rearrange("p (i o) -> p i o", o=1).broadcast_to((P, NT, CH)),
                            cst("slotno").rearrange("p (o n) -> p o n", o=1).broadcast_to((P, NT, CH)),
                            ALU.is_equal).then_inc(perm_ready, 1)
            tc = tmp[:, :].rearrange("p (c e) -> p c e", e=E)
            link(v.tensor_tensor(tc, cnt[:, 2, :].rearrange("p (o e) -> p o e", o=1).broadcast_to((P, NCH + 1, E)),
                                 cst("chunkno").rearrange("p (c e) -> p c e", e=E), ALU.is_le))
            link(v.tensor_reduce(meta[:, :], tc, AX, ALU.add))
            v.tensor_scalar(metai[:, 0:NCH + 1], meta[:, :], float(E - 1), None, ALU.min).then_inc(meta_ready, 1)
            v.tensor_copy(metai[:, NCH + 1:NCH + 2], cnt[:, 2, E - 1:E]).then_inc(meta_ready, 1)

            n_chunks = chunks_in_use(v)

            def keep_rows(c):
                v.wait_ge(xeT_mm, c + 1)
                v.tensor_copy(xeT[:, :, :].rearrange("p k n -> p (k n)"), bank[5][:, 0:2 * P]).then_inc(xeT_ready, 1)
                if isinstance(c, int) and c == 0:
                    v.wait_ge(xe_in, 16)
                v.tensor_copy(xk[:, ds(((c + 1) % 4) * ROW_W, ROW_W)], xe).then_inc(xk_ready, 1)

            def keep_hidden(done, before=None):
                for s in range(2):
                    v.wait_ge(gh_ready[s], done)
                    if before is not None and s == 0:
                        v.wait_ge(ey_mm, before)
                    v.tensor_copy(eh[:, 4 * s:4 * s + 4, :], gh[:, 4 * s:4 * s + 4, :]).then_inc(eh_ready[s], 1)

            def step(j, done, ins):
                ins.then_inc(estep[j], 1)
                v.wait_ge(estep[j], done)

            def finish(done):
                kept = (done % 4) * ROW_W
                at_step = [0]

                def link_step(ins):
                    step(at_step[0], done, ins)
                    at_step[0] += 1

                v.wait_ge(eout_room, done)
                v.wait_ge(ey_mm, done)
                v.scalar_tensor_tensor(out=ez, in0=bank[6][:, 0:D], scalar=xk[:, ds(kept + D, 1)],
                                       in1=xk[:, ds(kept, D)], op0=ALU.mult, op1=ALU.add).then_inc(y_room, 1)
                v.wait_ge(y_room, done + 1)
                link_step(v.bn_stats(est[:, 0:6], ez))
                v.tensor_scalar(est[:, 12:13], xk[:, ds(kept + D + 1, 1)], 0.0, 2.0 * TOK, ALU.is_equal, ALU.mult)
                link_step(v.bn_aggr(est[:, 6:8], est[:, 0:6]))
                inverse_root(v, link_step, est[:, 8:9], est[:, 9:10], est[:, 10:11], est[:, 11:12], est[:, 7:8])
                v.scalar_tensor_tensor(out=eti[:, :], in0=xk[:, ds(kept + D + 1, 1)], scalar=-1.0,
                                       in1=est[:, 12:13], op0=ALU.add, op1=ALU.add).then_inc(eout_ready, 1)
                v.tensor_scalar(eout, ez, est[:, 6:7], est[:, 9:10], ALU.subtract, ALU.mult).then_inc(eout_ready, 1)

            v.sem_inc(y_room, 1)
            v.sem_inc(eout_room, 1)
            keep_rows(0)
            keep_rows(1)
            keep_hidden(1)
            keep_rows(2)
            with v.Fori(1, NCH) as c:
                with v.If(c < n_chunks):
                    keep_hidden(c + 1, before=c)
                    finish(c)
                    with v.If(c + 1 < n_chunks):
                        keep_rows(c + 2)
            finish(n_chunks)

        @block.scalar
        def _(a):
            for i, (t0, n) in enumerate(TILES):
                a.wait_ge(tok_mm, i + 1)
                a.activation(res[0:n, i, :], bank[i][0:n, 0:D], ACT.Copy).then_inc(res_ready, 1)

            def affine_T(l, i, g, b):
                t0, n = TILES[i]
                a.wait_ge(nT_mm[l], i + 1)
                for k in range(KT):
                    last = a.activation(nT[:, k, t0:t0 + n], bank[5 + i % 2][:, k * P:k * P + n], ACT.Identity,
                                        scale=cols[:, g * KT + k:g * KT + k + 1],
                                        bias=cols[:, b * KT + k:b * KT + k + 1])
                last.then_inc(nT_ready[l], 1)

            def copy_qT(i):
                t0, n = TILES[i]
                a.wait_ge(qkT_mm, i + 1)
                for h in range(4):
                    a.activation(km[:, 1, h, t0:t0 + n], bank[4][:, 2 * P:2 * P + n], ACT.Copy,
                                 scale=cst("headmask")[:, h:h + 1])
                a.activation(qT[:, :, t0:t0 + n], bank[4][:, 0:2 * P].rearrange("p (t n) -> p t n", t=KT)[:, :, 0:n],
                             ACT.Copy).then_inc(qT_ready, 1)

            a.wait_ge(const_in, 32)
            affine_T(0, 0, 0, 1)
            affine_T(0, 1, 0, 1)
            for i in range(NT):
                if i + 2 < NT:
                    affine_T(0, i + 2, 0, 1)
                if i >= 1:
                    copy_qT(i - 1)
            copy_qT(NT - 1)

            def exps(p):
                a.wait_ge(dif_ready, p + 1)
                if p == 0:
                    a.wait_ge(rope_ready, NT)
                    a.wait_ge(qkT_mm, NT)
                if p >= 2:
                    a.wait_ge(pT_mm, p - 1)
                a.activation(prob[:, p % 2, :], dif[:, p % 2, :], ACT.Exp, scale=float(HD) ** -0.5)\
                    .then_inc(prob_ready, 1)

            def copy_pT(p):
                a.wait_ge(pT_mm, p + 1)
                if p >= 2:
                    a.wait_ge(av_mm, p - 1)
                full = len(GROUPS) - 1
                a.activation(pT[0:HG * SEQ, p % 2, 0:full, :].rearrange("p g n -> p (g n)"),
                             bank45[0:HG * SEQ, 0:full * P], ACT.Copy)
                nh = GROUPS[full][1]
                a.activation(pT[0:nh * SEQ, p % 2, full, :], bank45[0:nh * SEQ, full * P:(full + 1) * P],
                             ACT.Copy).then_inc(pT_ready, 1)

            def copy_oT(p):
                a.wait_ge(oT_mm, p + 1)
                src = bank67[:, :].rearrange("p (t n) -> p t n", t=KT)[:, :, OT_AT:OT_AT + P]\
                    .rearrange("p t (i q) -> p t i q", i=2)[:, :, :, 0:SEQ]
                dst = oT[:, :, 2 * p * SEQ:(2 * p + 2) * SEQ].rearrange("p t (i q) -> p t i q", i=2)
                a.activation(dst, src, ACT.Copy).then_inc(oT_ready, 1)

            for p in range(PAIRS + 3):
                if p >= 3:
                    copy_oT(p - 3)
                if 1 <= p <= PAIRS:
                    copy_pT(p - 1)
                if p < PAIRS:
                    exps(p)

            HT = TOK // 2
            half_tiles = [-(-HT * (s + 1) // P) for s in range(2)]
            for i in range(half_tiles[0]):
                affine_T(1, i, 2, 3)
            for q in range(2 * FT):
                s, j = divmod(q, FT)
                if q == FT - 3:
                    for i in range(half_tiles[0], NT):
                        affine_T(1, i, 2, 3)
                a.wait_ge(up_mm, q + 1)
                a.activation(hidT[:, j, s * HT:(s + 1) * HT], bank[q % 4][:, 0:HT], ACT.Gelu,
                             bias=cols[:, 4 * KT + j:4 * KT + j + 1]).then_inc(hid_ready, 1)
            for i, (t0, n) in enumerate(TILES):
                a.wait_ge(nT_mm[2], i + 1)
                a.activation(nT[:, :, t0:t0 + n],
                             bank[1 + i % 2][:, 0:2 * P].rearrange("p (t n) -> p t n", t=KT)[:, :, 0:n], ACT.Copy)\
                    .then_inc(nT_ready[2], 1)
            a.wait_ge(shift_ready, 1)
            a.activation(lg[:, :, :], lg[:, :, :], ACT.Exp).then_inc(expl_ready, 1)

            n_chunks = chunks_in_use(a)

            def stage(s, e):
                a.activation(w1s[:, 4 * s:4 * s + 4, :].rearrange("p k n -> p (k n)"),
                             we[:, ds(e * EXP_W + s * KT * 512, KT * 512)], ACT.Copy).then_inc(w1s_ready[s], 1)

            def stage_bias(e):
                a.activation(b1s[:, :], b1[:, ds(e * FT, FT)], ACT.Copy).then_inc(b1s_ready, 1)

            def gelu(c, first):
                e = expert_of(c + 1)
                a.wait_ge(b1s_ready, c + 1)
                for s in range(2):
                    a.wait_ge(eup_mm[s], c + 1)
                    stage(s, e)
                    if not first:
                        a.wait_ge(eh_ready[s], c)
                    for j in range(4):
                        last = a.activation(gh[:, 4 * s + j, :], bank[s][:, j * P:(j + 1) * P], ACT.Gelu,
                                            bias=b1s[:, 4 * s + j:4 * s + j + 1])
                    last.then_inc(gh_ready[s], 1)
                a.wait_ge(gh_ready[1], c + 1)
                stage_bias(e)

            def expert_of(c):
                return a.value_load(metai[0:1, ds(c, 1)], min_val=0, max_val=E - 1)

            a.wait_ge(b1_in, 16)
            for e in range(E):
                a.wait_ge(we_in[e], 16)
            for s in range(2):
                stage(s, expert_of(0))
            stage_bias(expert_of(0))
            gelu(0, True)
            with a.Fori(1, NCH) as c:
                with a.If(c < n_chunks):
                    gelu(c, False)

        @block.gpsimd
        def _(g):
            g.memset(zero, 0.0).then_inc(zero_ready, 1)
            g.wait_ge(const_in, 32)
            g.tensor_copy(beforeb[:, :], cst("before")).then_inc(bf_ready, 1)
            g.tensor_copy(onesb[:, :], cst("ones")).then_inc(bf_ready, 1)
            g.tensor_copy(caus[:, :], cst("causal")).then_inc(mask_ready, 1)
            g.tensor_copy(id64[:, :], cst("id64")).then_inc(mask_ready, 1)
            g.memset(qT[:, :, TOK:QTW], 0.0).then_inc(qpad_ready, 1)
            for i, (t0, n) in enumerate(TILES):
                g.wait_ge(qk_ready, i + 1)
                if i >= 2:
                    g.wait_ge(qkT_mm, i - 1)
                cs = cst("cos")[0:n, i * HD:(i + 1) * HD].rearrange("p (o c) -> p o c", o=1).broadcast_to((n, 2 * H, HD))
                g.tensor_tensor(ropec[0:n, i % 2, :].rearrange("p (h c) -> p h c", c=HD),
                                qk[0:n, i % 2, :].rearrange("p (h c) -> p h c", c=HD), cs, ALU.mult)\
                    .then_inc(ropec_ready, 1)
                g.wait_ge(ropec_ready, i + 1)
                g.wait_ge(ropes_ready, i + 1)
                g.tensor_tensor(ropec[0:n, i % 2, :], ropec[0:n, i % 2, :], ropes[0:n, i % 2, :],
                                ALU.add).then_inc(rope_ready, 1)
            R = HG * SEQ
            vm = cst("vmask")[0:R, :].rearrange("p (i o c) -> p i o c", i=1, c=VW)
            g.tensor_copy(vb[0:R, :, 0:H, HD], vm[:, :, :, HD].broadcast_to((R, IMGS, H)))
            g.memset(vb[0:R, :, H:HO, 0:HD], 0.0)
            g.memset(vb[0:R, :, H:HO, HD], 1.0).then_inc(vb_ready, 1)
            for p in range(PAIRS):
                if p == 0:
                    g.wait_ge(vrep_in[0], 16 * HG)
                if 2 * p == EARLY_IMGS:
                    g.wait_ge(vrep_in[1], 16 * HG)
                src = vrep[0:R, 2 * p:2 * p + 2, :].rearrange("p i (o c) -> p i o c", c=HD)
                g.tensor_tensor(vb[0:R, 2 * p:2 * p + 2, 0:H, 0:HD], src, vm[:, :, :, 0:HD].broadcast_to((R, 2, H, HD)), ALU.mult)\
                    .then_inc(vb_ready, 1)
            g.wait_ge(eb_in, 16)
            for s in range(3):
                g.tensor_copy(ebp[:, s, :], ebf[:, s, :]).then_inc(eb_split, 1)
                g.wait_ge(eb_split, s + 1)
                if s < 2:
                    g.tensor_tensor(ebf[:, s + 1, :], ebf[:, s, :], ebp[:, s, :], ALU.subtract).then_inc(eb_rest, 1)
                    g.wait_ge(eb_rest, s + 1)
            for i, (t0, n) in enumerate(TILES):
                g.wait_ge(res_ready, i + 1)
                g.tensor_tensor(mid[0:n, i, :], res[0:n, i, :], rows[0:n, 3 * D:4 * D], ALU.add).then_inc(mid_ready, 1)
            for i, (t0, n) in enumerate(TILES):
                g.wait_ge(x2_ready, i + 1)
                g.tensor_tensor(res[0:n, i, :], res[0:n, i, :], x2[0:n, i, :], ALU.add).then_inc(pl, 1)
                g.wait_ge(pl, i + 1)
                g.tensor_tensor(res[0:n, i, :], res[0:n, i, :], rows[0:n, 4 * D:5 * D], ALU.add).then_inc(hx_ready, 1)
            g.wait_ge(row_ready, 1)
            g.wait_ge(pay_ready, 2)
            g.wait_ge(rows_cleared, 16)
            for i, (t0, n) in enumerate(TILES):
                g.indirect_dma_start(xs_dram, bass.IndirectOffsetOnAxis(rowi[0:n, i:i + 1], 0), pay[0:n, i, :], None)\
                    .then_inc(xs_out, 16)
            n_chunks = chunks_in_use(g)

            def store(done):
                g.wait_ge(eout_ready, 2 * done)
                g.sem_inc(store_begun, 1)
                g.indirect_dma_start(out_d, bass.IndirectOffsetOnAxis(eti[:, 0:1], 0), eout, None,
                                     bounds_check=TOK - 1, oob_is_err=False).then_inc(out_st, 16)
                g.wait_ge(out_st, 16 * done)
                g.sem_inc(eout_room, 1)

            store(1)
            with g.Fori(2, NCH + 1) as c:
                with g.If(c < n_chunks + 1):
                    store(c)


def kernel(x, L0_tok_W, L0_attn_ln1_g, L0_attn_ln1_b, L0_attn_Wqkv, L0_attn_bqkv, L0_attn_Wo, L0_attn_bo,
           L0_attn_ln2_g, L0_attn_ln2_b, L0_attn_W1, L0_attn_b1, L0_attn_W2, L0_attn_b2, L0_ffn_W1, L0_ffn_b1,
           L0_ffn_W2, L0_ffn_b2, L0_ffn_Wr, L0_ffn_br):
    import concourse.bacc as bacc
    from concourse.bass_utils import run_bass_kernel_spmd

    def on_partitions(w):
        w = np.asarray(w)
        return w.reshape(-1, P, w.shape[-1]).transpose(1, 0, 2)

    heads = [t * 8 + half * 4 + h4 for half in range(2) for t in range(2) for h4 in range(4)]
    slot_cols = np.concatenate([np.arange(h * HD, (h + 1) * HD) for h in heads])
    qkv_cols = np.concatenate([np.arange(2 * D), 2 * D + slot_cols])

    patches = np.asarray(x).reshape(IMGS, 3, 6, 16, 6, 16).transpose(0, 1, 3, 5, 2, 4).reshape(TOK, 3 * 256).T
    w1e, w2e = np.asarray(L0_ffn_W1), np.asarray(L0_ffn_W2)
    experts = np.concatenate([w1e.reshape(E, KT, P, 2, F // 2).transpose(0, 2, 3, 1, 4).reshape(E, P, KT * F),
                              w2e.reshape(E, FT, P, D).transpose(0, 2, 1, 3).reshape(E, P, FT * D)], axis=2)
    rows = np.concatenate([np.asarray(L0_attn_bqkv)[qkv_cols], np.asarray(L0_attn_bo), np.asarray(L0_attn_b2),
                           np.asarray(L0_ffn_br)])[None, :]
    cols = np.concatenate([np.asarray(a).reshape(-1, P).T for a in
                           (L0_attn_ln1_g, L0_attn_ln1_b, L0_attn_ln2_g, L0_attn_ln2_b, L0_attn_b1)], axis=1)
    arrays = {
        "xT": on_partitions(patches), "tokw": on_partitions(L0_tok_W),
        "wqkv": on_partitions(np.asarray(L0_attn_Wqkv)[:, qkv_cols]),
        "wo": on_partitions(np.asarray(L0_attn_Wo)[slot_cols]), "w1": on_partitions(L0_attn_W1),
        "w2": on_partitions(L0_attn_W2), "we": experts, "wr": on_partitions(L0_ffn_Wr),
        "b1": np.asarray(L0_ffn_b1).reshape(E * FT, P).T, "rows": rows, "cols": cols,
        "eb": np.asarray(L0_ffn_b2).reshape(P, -1), "consts": shape_constants(),
    }
    nc = bacc.Bacc("TRN2", target_bir_lowering=False, num_devices=1)
    arrays = {k: np.ascontiguousarray(a) for k, a in arrays.items()}
    args = [nc.dram_tensor(k + "_in", a.shape, F32, kind="ExternalInput").ap() for k, a in arrays.items()]
    out = nc.dram_tensor("out", (TOK, D), F32, kind="ExternalOutput").ap()
    tower(nc, *args, out)
    r = run_bass_kernel_spmd(nc, [{k + "_in": a for k, a in arrays.items()}], core_ids=[0])
    return r.results[0]["out"].reshape(IMGS, SEQ, D)
```

```python
from contextlib import ExitStack

import numpy as np
import concourse.bass as bass
from concourse.bass import ds
from concourse import mybir

ALU = mybir.AluOpType
ACT = mybir.ActivationFunctionType
F32 = mybir.dt.float32
BF16 = mybir.dt.bfloat16
I32 = mybir.dt.int32
AX = mybir.AxisListType.X

P = 128
IMGS, SEQ, D, H, HD = 16, 36, 256, 16, 16
TOK = IMGS * SEQ
KT = D // P
TILES = [(t, min(P, TOK - t)) for t in range(0, TOK, P)]
NT = len(TILES)
PATCH_K = 3 * 16 * 16 // P
F = 1024
FT = F // P
E = 8
PAIRS = IMGS // 2
EARLY_IMGS = 2 * P // SEQ // 2 * 2
HG = 3
GROUPS = [(o, min(HG, H - o)) for o in range(0, H, HG)]
VW = HD + 1
PARTS = ((0, 2 * P), (2 * P, TOK))
LATE = NT - 2
HB = 3 * HG
OT_AT = 2 * HB * VW
HO = 2 * HB
CH = P
NCH = (TOK - E) // CH + E
EXP_W = KT * F + FT * D
ROW_W = D + 2
EPS = 1e-5
NEG = -1e30


def const_layout():
    at, out = 0, {}
    for name, w in (("ident", P), ("headmask", 4), ("cos", NT * HD), ("sin", NT * HD), ("before", P), ("ones", P),
                    ("vmask", H * VW), ("causal", 8 * SEQ), ("id64", 64), ("tokno", NT), ("thr", E * NT),
                    ("earlier", E * E), ("chunkno", (NCH + 1) * E), ("slotno", CH), ("eidx", E)):
        out[name] = (at, at + w)
        at += w
    return out, at


def shape_constants():
    lay, width = const_layout()
    c = np.zeros((P, width), np.float32)
    p = np.arange(P)

    def put(name, a):
        lo, hi = lay[name]
        c[:, lo:hi] = np.broadcast_to(a, (P,) + a.shape[1:]).reshape(P, hi - lo)

    put("ident", np.eye(P))
    put("headmask", ((p[:, None] % 64) // HD == np.arange(4)[None, :]).astype(np.float32))
    inv = 1.0 / 10000.0 ** (np.arange(0, HD, 2, dtype=np.float32) / np.float32(HD))
    pos = ((p[:, None] + P * np.arange(NT)[None, :]) % SEQ).astype(np.float32)
    ang = pos[:, :, None] * np.concatenate([inv, inv]).astype(np.float32)[None, None, :]
    sign = np.where(np.arange(HD) < HD // 2, -1.0, 1.0)
    put("cos", np.cos(ang))
    put("sin", np.sin(ang) * sign)
    put("before", (p[:, None] < p[None, :]).astype(np.float32))
    put("ones", np.ones((P, P)))
    vm = (p[:, None] // SEQ == np.arange(H)[None, :] % HG).astype(np.float32)
    put("vmask", np.repeat(vm, VW, axis=1))
    q = p % 64
    ca = np.where((q[:, None] < SEQ) & (np.arange(SEQ)[None, :] > q[:, None]), NEG, 0.0)
    put("causal", np.tile(ca, (1, 8)))
    put("id64", (q[:, None] == np.arange(64)[None, :]).astype(np.float32))
    put("tokno", p[:, None] + P * np.arange(NT)[None, :] + 1.0)
    put("thr", np.tile(CH * np.arange(NT), E)[None, :])
    put("earlier", (np.arange(E)[None, :] < np.arange(E)[:, None]).astype(np.float32).reshape(1, -1))
    put("chunkno", np.repeat(np.arange(NCH + 1), E)[None, :])
    put("slotno", np.arange(CH)[None, :])
    put("eidx", np.arange(E)[None, :])
    return c


def tower(nc, xT_d, tokw_d, wqkv_d, wo_d, w1_d, w2_d, we_d, wr_d, b1_d, rows_d, cols_d, eb_d, const_d, out_d):
    ctx = ExitStack()
    with ctx:
        def sb(name, shape, dt=F32):
            return ctx.enter_context(nc.sbuf_tensor(name, shape, dt))

        def sem(name):
            return ctx.enter_context(nc.semaphore(name))

        lay, cw = const_layout()
        const = sb("const", [P, cw])

        def cst(name):
            return const[:, lay[name][0]:lay[name][1]]

        ident = cst("ident")
        xs_dram = nc.dram_tensor("chunk_rows", [(NCH + 1) * CH, ROW_W], F32, kind="Internal").ap()
        eb_dram = nc.dram_tensor("expert_bias_parts", [3, E * D], BF16, kind="Internal").ap()
        v_dram = nc.dram_tensor("v_scratch", [TOK, D], F32, kind="Internal").ap()

        RES = 2
        we = sb("expert_w", [P, E * EXP_W])
        early = we[:, RES * EXP_W:E * EXP_W]
        at = [0]

        def carve(n):
            at[0] += n
            assert at[0] <= (E - RES) * EXP_W
            return early[:, at[0] - n:at[0]]

        dif = carve(2 * H * SEQ).rearrange("p (b n) -> p b n", b=2)
        prob = carve(2 * H * SEQ).rearrange("p (b n) -> p b n", b=2)
        vb = carve(IMGS * HO * VW).rearrange("p (i o c) -> p i o c", i=IMGS, o=HO)
        vrep = carve(IMGS * D).rearrange("p (i c) -> p i c", i=IMGS)
        tokw = carve(PATCH_K * D).rearrange("p (k n) -> p k n", k=PATCH_K)
        wqkv = carve(KT * 3 * D).rearrange("p (k n) -> p k n", k=KT)
        assert at[0] <= 4 * EXP_W
        at[0] = 4 * EXP_W
        km_f = carve(KT * 4 * TOK)
        km = km_f.rearrange("p (t h n) -> p t h n", t=KT, h=4)
        xT = km_f[:, 0:PATCH_K * TOK].rearrange("p (k n) -> p k n", k=PATCH_K)
        wo = sb("wo", [P, KT, D])
        w1 = carve(KT * F).rearrange("p (k n) -> p k n", k=KT)
        w2 = sb("w2", [P, FT, D])
        wr = sb("wr", [P, KT, E])
        b1 = sb("b1", [P, E * FT])
        b1s = sb("b1s", [P, FT])
        rows = sb("rows", [P, 5 * D + E])
        cols = sb("cols", [P, 4 * KT + FT])
        res = sb("res", [P, NT, D])
        mid = sb("mid", [P, NT, D])
        pay = sb("pay", [P, NT, ROW_W])
        x2 = carve(NT * D).rearrange("p (i c) -> p i c", i=NT)
        nT = sb("nT", [P, KT, TOK])
        oT = nT
        bst = sb("bst", [P, NT, 6])
        mv = sb("mv", [P, NT, 2])
        nw = sb("nw", [P, 4, NT])
        scr = sb("scr", [P, 6336 + 2 * HO * HD])
        nrm = [x2, scr[:, 0:NT * D].rearrange("p (i c) -> p i c", i=NT), pay]
        qk = scr[:, 0:1024].rearrange("p (b n) -> p b n", b=2)
        ropec = scr[:, 1024:2048].rearrange("p (b n) -> p b n", b=2)
        ropes = scr[:, 2048:3072].rearrange("p (b n) -> p b n", b=2)
        vt = mid
        QTW = TOK + 32
        qT = scr[:, 3584:3584 + KT * QTW].rearrange("p (t n) -> p t n", t=KT)
        pT = scr[:, 4800:4800 + 1536].rearrange("p (b g n) -> p b g n", b=2, g=len(GROUPS))
        on = scr[:, 6336:6336 + 2 * HO * HD].rearrange("p (b n) -> p b n", b=2)
        xe = scr[:, 0:ROW_W]
        xeT = scr[:, ROW_W:ROW_W + D].rearrange("p (k n) -> p k n", k=KT)
        hidT = scr[:, 2304:2304 + FT * TOK].rearrange("p (k n) -> p k n", k=FT)
        gh = scr[:, 3072:3072 + F].rearrange("p (k n) -> p k n", k=FT)
        eh = scr[:, 3072 + F:3072 + 2 * F].rearrange("p (k n) -> p k n", k=FT)
        w1s = w2
        perm = nT[:, :, :].rearrange("p k n -> p (k n)")[:, 0:NT * CH].rearrange("p (i n) -> p i n", i=NT)
        ez = [res[:, b, :] for b in (0, 2)]
        eout = [res[:, b, :] for b in (1, 3, 4)]
        xk = mid[:, :, :].rearrange("p i c -> p (i c)")
        ebr = scr[0:3, NT * D:NT * D + E * D // 2].bitcast(BF16)
        zero = pay[:, 0, :]
        est = sb("est", [P, 2, 16])
        eti = sb("eti", [P, 3], I32)
        EBP = E * D // P
        ebf = sb("ebf", [P, 3, EBP])
        ebp = sb("ebp", [P, 3, EBP], BF16)
        lg = sb("lg", [P, NT, E])
        lmax = sb("lmax", [P, NT])
        first = sb("first", [P, NT, E])
        gate = sb("gate", [P, NT])
        onehot = sb("onehot", [P, NT, E])
        onehotb = sb("onehotb", [P, NT, E], BF16)
        beforeb = sb("beforeb", [P, P], BF16)
        onesb = sb("onesb", [P, P], BF16)
        cnt = sb("cnt", [P, 4, E])
        tmp = sb("tmp", [P, (NCH + 1) * E])
        table = sb("table", [P, 1])
        meta = sb("meta", [P, NCH + 1])
        metai = sb("metai", [P, NCH + 2], I32)
        row = sb("row", [P, NT])
        rowi = sb("rowi", [P, NT], I32)
        mx = sb("mx", [P, 2, H])
        rinv = sb("rinv", [P, 2, HO])
        caus = sb("caus", [P, 8 * SEQ], BF16)
        id64 = sb("id64b", [P, 64], BF16)

        score = [ctx.enter_context(nc.psum_tensor(f"bank{b}{b + 1}", [P, 1024], F32)) for b in (0, 2)]
        bank = [score[b // 2][:, (b % 2) * 512:(b % 2 + 1) * 512] for b in range(4)]
        bank45 = ctx.enter_context(nc.psum_tensor("bank45", [P, 1024], F32))
        bank += [bank45[:, 0:512], bank45[:, 512:1024]]
        bank67 = ctx.enter_context(nc.psum_tensor("bank67", [P, 1024], F32))
        bank += [bank67[:, 0:512], bank67[:, 512:1024]]

        xt_in = [sem(f"xt_in{k}") for k in range(PATCH_K)]
        const_in = sem("const_in")
        rows_in = sem("rows_in")
        wqkv_in = sem("wqkv_in")
        mlp_in = sem("mlp_in")
        vt_out = [sem(f"vt_out{i}") for i in range(NT)]
        vrep_in = [sem(f"vrep_in{s}") for s in range(2)]
        out_st = sem("out_st")
        tok_mm = sem("tok_mm")
        res_ready = sem("res_ready")
        dve = sem("dve")
        pl = sem("pl")
        nrm_ready = [sem(f"nrm_ready{l}") for l in range(3)]
        nT_mm = [sem(f"nT_mm{l}") for l in range(3)]
        nT_ready = [sem(f"nT_ready{l}") for l in range(3)]
        qk_mm = sem("qk_mm")
        v_mm = sem("v_mm")
        qk_ready = sem("qk_ready")
        ropec_ready = sem("ropec_ready")
        ropes_ready = sem("ropes_ready")
        rope_ready = sem("rope_ready")
        vt_ready = sem("vt_ready")
        qkT_mm = sem("qkT_mm")
        qT_ready = sem("qT_ready")
        km_ready = sem("km_ready")
        qpad_ready = sem("qpad_ready")
        mask_ready = sem("mask_ready")
        vb_ready = sem("vb_ready")
        score_mm = sem("score_mm")
        dif_ready = sem("dif_ready")
        prob_ready = sem("prob_ready")
        pT_mm = sem("pT_mm")
        pT_ready = sem("pT_ready")
        av_mm = sem("av_mm")
        on_ready = sem("on_ready")
        oT_mm = sem("oT_mm")
        oT_ready = sem("oT_ready")
        mid_ready = sem("mid_ready")
        wo_mm = sem("wo_mm")
        x2_ready = sem("x2_ready")
        hx_ready = sem("hx_ready")
        up_mm = sem("up_mm")
        hid_ready = sem("hid_ready")
        down_mm = sem("down_mm")
        x3_ready = sem("x3_ready")
        we_in = [sem(f"we_in{e}") for e in range(E)]
        b1_in = sem("b1_in")
        eb_in = sem("eb_in")
        eb_split = sem("eb_split")
        eb_rest = sem("eb_rest")
        ebp_out = sem("ebp_out")
        ebr_in = sem("ebr_in")
        zero_ready = sem("zero_ready")
        rows_cleared = sem("rows_cleared")
        bf_ready = sem("bf_ready")
        logit_mm = sem("logit_mm")
        shift_ready = sem("shift_ready")
        expl_ready = sem("expl_ready")
        onehot_ready = sem("onehot_ready")
        rank_mm = sem("rank_mm")
        stat_ready = sem("stat_ready")
        root_ready = sem("root_ready")
        row_ready = sem("row_ready")
        pay_ready = sem("pay_ready")
        meta_ready = sem("meta_ready")
        xs_out = sem("xs_out")
        x0_in = sem("x0_in")
        xe_in = sem("xe_in")
        xeT_mm = sem("xeT_mm")
        xeT_ready = sem("xeT_ready")
        perm_ready = sem("perm_ready")
        rows0_mm = sem("rows0_mm")
        rows0_ready = sem("rows0_ready")
        b1s_ready = sem("b1s_ready")
        w1s_ready, eup_mm, gh_ready, eh_ready = ([sem(f"{name}{s}") for s in range(2)] for name in
                                                 ("w1s_ready", "eup_mm", "gh_ready", "eh_ready"))
        ey_mm = sem("ey_mm")
        xk_ready = sem("xk_ready")
        y_room = sem("y_room")
        eout_ready = sem("eout_ready")
        store_begun = sem("store_begun")
        eout_room = sem("eout_room")
        estep = [sem(f"estep{j}") for j in range(14)]

        block = ctx.enter_context(nc.Block())

        def inverse_root(eng, link, vh, y, a, b, var, fused=True):
            link(eng.tensor_scalar(vh, var, EPS, -0.5, ALU.add, ALU.mult))
            link(eng.tensor_scalar(y.bitcast(I32), vh.bitcast(I32), -0.5, float(0x5F3759DF - 0x40400000),
                                   ALU.mult, ALU.add))
            for _ in range(3):
                if fused and y.shape[1] == 1:
                    link(eng.scalar_tensor_tensor(out=b, in0=y, scalar=y, in1=vh, op0=ALU.mult, op1=ALU.mult))
                else:
                    link(eng.tensor_tensor(a, y, y, ALU.mult))
                    link(eng.tensor_tensor(b, a, vh, ALU.mult))
                if fused:
                    link(eng.scalar_tensor_tensor(out=y, in0=b, scalar=1.5, in1=y, op0=ALU.add, op1=ALU.mult))
                else:
                    link(eng.tensor_scalar(b, b, 1.5, None, ALU.add))
                    link(eng.tensor_tensor(y, b, y, ALU.mult))

        def chunks_in_use(eng):
            eng.wait_ge(meta_ready, 2)
            return eng.value_load(metai[0:1, NCH + 1:NCH + 2], min_val=1, max_val=NCH)

        @block.sync
        def _(sp):
            for k in range(PATCH_K):
                sp.dma_start(xT[:, k, :], xT_d[:, k, :]).then_inc(xt_in[k], 16)
                sp.dma_start(tokw[:, k, :], tokw_d[:, k, :]).then_inc(xt_in[k], 16)
            sp.dma_start(const[:, :], const_d).then_inc(const_in, 16)
            sp.dma_start(cols[:, :], cols_d).then_inc(const_in, 16)
            sp.dma_start(rows[:, :], rows_d.broadcast_to((P, 5 * D + E))).then_inc(rows_in, 16)
            sp.dma_start(wqkv[:, :, :], wqkv_d).then_inc(wqkv_in, 16)
            sp.dma_start(wo[:, :, :], wo_d).then_inc(mlp_in, 16)
            sp.dma_start(w1[:, :, :], w1_d).then_inc(mlp_in, 16)
            sp.dma_start(w2[:, :, :], w2_d).then_inc(mlp_in, 16)
            sp.dma_start(wr[:, :, :], wr_d).then_inc(mlp_in, 16)
            sp.dma_start(b1[:, :], b1_d).then_inc(b1_in, 16)
            sp.dma_start(ebf[:, 0, :], eb_d).then_inc(eb_in, 16)
            sp.wait_ge(zero_ready, 1)
            sp.dma_start(xs_dram.rearrange("(c p) d -> p c d", p=CH),
                         zero.rearrange("p (o d) -> p o d", o=1).broadcast_to((P, NCH + 1, ROW_W)))\
                .then_inc(rows_cleared, 16)
            for i, (t0, n) in enumerate(TILES):
                sp.wait_ge(vt_ready, i + 1)
                sp.dma_start(v_dram[t0:t0 + n, :], vt[0:n, i, :]).then_inc(vt_out[i], 16)
                if i in (2, NT - 1):
                    part = 0 if i == 2 else 1
                    lo, hi = (0, EARLY_IMGS) if part == 0 else (EARLY_IMGS, IMGS)
                    for t in range(2) if part == 0 else range(2, NT):
                        sp.wait_ge(vt_out[t], 16)
                    for j in range(HG):
                        sp.dma_start(vrep[SEQ * j:SEQ * (j + 1), lo:hi, :],
                                     v_dram.rearrange("(i k) c -> k i c", k=SEQ)[:, lo:hi, :])\
                            .then_inc(vrep_in[part], 16)
            for e in range(RES):
                sp.dma_start(we[:, e * EXP_W:(e + 1) * EXP_W], we_d[e]).then_inc(we_in[e], 16)
            sp.wait_ge(eb_split, 3)
            sp.dma_start(eb_dram.rearrange("s (p c) -> p s c", p=P), ebp[:, :, :]).then_inc(ebp_out, 16)
            sp.wait_ge(av_mm, PAIRS)
            sp.wait_ge(ebp_out, 16)
            for e in range(RES, E - 1):
                sp.dma_start(we[:, e * EXP_W:(e + 1) * EXP_W], we_d[e]).then_inc(we_in[e], 16)
            sp.wait_ge(oT_ready, PAIRS)
            sp.dma_start(ebr, eb_dram).then_inc(ebr_in, 16)
            sp.wait_ge(up_mm, 2 * FT)
            sp.wait_ge(hx_ready, NT)
            for e in range(E - 1, E):
                sp.dma_start(we[:, e * EXP_W:(e + 1) * EXP_W], we_d[e]).then_inc(we_in[e], 16)
            n_chunks = chunks_in_use(sp)
            sp.wait_ge(xs_out, 16 * NT)
            sp.dma_start(xk[:, ROW_W:2 * ROW_W], xs_dram[0:CH, :]).then_inc(x0_in, 16)
            sp.dma_start(xe, xs_dram[CH:2 * CH, :]).then_inc(xe_in, 16)
            with sp.Fori(2, NCH + 1) as c:
                with sp.If(c < n_chunks + 1):
                    sp.wait_ge(xeT_mm, c)
                    sp.wait_ge(xk_ready, c)
                    sp.dma_start(xe, xs_dram[ds(c * CH, CH), :]).then_inc(xe_in, 16)

        @block.tensor
        def _(pe):
            def transpose_tile(l, i):
                t0, n = TILES[i]
                b = bank[(1 if l == 2 else 5) + i % 2]
                pe.wait_ge(nrm_ready[l], i + 1)
                if i >= 2:
                    pe.wait_ge(nT_ready[l], i - 1)
                for k in range(KT):
                    last = pe.transpose(b[:, k * P:k * P + n], nrm[l][0:n, i, k * P:(k + 1) * P], ident[0:n, 0:n])
                last.then_inc(nT_mm[l], 1)

            def embed(i, k):
                t0, n = TILES[i]
                last = pe.matmul(bank[i][0:n, 0:D], xT[:, k, t0:t0 + n], tokw[:, k, :],
                                 start=(k == 0), stop=(k == PATCH_K - 1))
                if k == PATCH_K - 1:
                    last.then_inc(tok_mm, 1)

            for k in range(PATCH_K // 3):
                pe.wait_ge(xt_in[k], 32)
                for i in range(NT):
                    embed(i, k)
            for i in range(NT):
                if i == NT - 1:
                    pe.wait_ge(const_in, 32)
                    transpose_tile(0, 0)
                for k in range(PATCH_K // 3, PATCH_K):
                    if i == 0:
                        pe.wait_ge(xt_in[k], 32)
                    embed(i, k)

            def project_qk(i):
                t0, n = TILES[i]
                pe.wait_ge(nT_ready[0], i + 1)
                if i == 0:
                    pe.wait_ge(wqkv_in, 16)
                if i < 2:
                    pe.wait_ge(res_ready, 2 * i + 2)
                if i >= 2:
                    pe.wait_ge(qk_ready, i - 1)
                    pe.wait_ge(vt_ready, i - 1)
                for k in range(KT):
                    last = pe.matmul(bank[2 * (i % 2)][0:n, :], nT[:, k, t0:t0 + n], wqkv[:, k, 0:2 * D],
                                     start=(k == 0), stop=(k == KT - 1))
                last.then_inc(qk_mm, 1)

            def project_v(i):
                t0, n = TILES[i]
                dst = bank[6 if i == NT - 1 else 2 * (i % 2) + 1]
                for k in range(KT):
                    last = pe.matmul(dst[0:n, 0:D], nT[:, k, t0:t0 + n], wqkv[:, k, 2 * D:3 * D],
                                     start=(k == 0), stop=(k == KT - 1))
                last.then_inc(v_mm, 1)

            def turn_qk(i):
                t0, n = TILES[i]
                pe.wait_ge(rope_ready, i + 1)
                if i == 0:
                    pe.wait_ge(res_ready, NT)
                else:
                    pe.wait_ge(qT_ready, i)
                    pe.wait_ge(km_ready, i)
                for j, dst in enumerate((bank[4][:, 0:P], bank[4][:, P:2 * P], bank[7][:, 0:P], bank[4][:, 2 * P:3 * P])):
                    last = pe.transpose(dst[:, 0:n], ropec[0:n, i % 2, j * P:(j + 1) * P], ident[0:n, 0:n])
                last.then_inc(qkT_mm, 1)

            transpose_tile(0, 1)
            for i in range(NT):
                project_qk(i)
                if i < NT - 1:
                    project_v(i)
                if i + 2 < NT:
                    transpose_tile(0, i + 2)
                if i >= 2:
                    turn_qk(i - 2)
            def scores(p):
                tiles = -(-min((2 * p + 1) * SEQ + 64, TOK) // P)
                pe.wait_ge(qT_ready, tiles)
                pe.wait_ge(km_ready, tiles)
                if p == 0:
                    pe.wait_ge(mask_ready, 2)
                    pe.wait_ge(qk_ready, NT)
                    pe.wait_ge(vt_ready, NT - 1)
                if p == PAIRS - 1:
                    pe.wait_ge(qpad_ready, 1)
                if p >= 2:
                    pe.wait_ge(dif_ready, p - 1)
                for half in range(2):
                    r = slice(64 * half, 64 * half + 64)
                    for im in range(2):
                        pe.matmul(bank[2 * (p % 2) + half][64 * im:64 * im + 64, 0:8 * SEQ], id64[r, :], caus[r, :],
                                  start=True, stop=False, skip_group_check=True)
                for t in range(KT):
                    for half in range(2):
                        r = slice(64 * half, 64 * half + 64)
                        for im in range(2):
                            q0 = (2 * p + im) * SEQ
                            last = pe.matmul(bank[2 * (p % 2) + half][64 * im:64 * im + 64,
                                                                      t * 4 * SEQ:(t + 1) * 4 * SEQ],
                                             qT[r, t, q0:q0 + 64], km[r, t, :, q0:q0 + SEQ],
                                             start=False, stop=True, skip_group_check=True)
                last.then_inc(score_mm, 1)

            def turn_probs(p):
                pe.wait_ge(prob_ready, p + 1)
                if p >= 1:
                    pe.wait_ge(pT_ready, p)
                else:
                    pe.wait_ge(nT_ready[0], NT)
                    pe.wait_ge(qT_ready, NT)
                    pe.wait_ge(km_ready, NT)
                for g, (o, nh) in enumerate(GROUPS):
                    last = pe.transpose(bank45[0:nh * SEQ, g * P:(g + 1) * P],
                                        prob[:, p % 2, o * SEQ:(o + nh) * SEQ], ident)
                last.then_inc(pT_mm, 1)

            def values(p):
                pe.wait_ge(pT_ready, p + 1)
                pe.wait_ge(vb_ready, p + 2)
                if p == 0:
                    pe.wait_ge(vt_ready, NT)
                if 1 <= p < PAIRS - 1:
                    pe.wait_ge(on_ready, p)
                    pe.wait_ge(oT_ready, p)
                for g, (o, nh) in enumerate(GROUPS):
                    dst = bank[(4 if p == PAIRS - 1 else 6) + g // 3][:, 0:2 * HB * VW].rearrange("p (i n) -> p i n", i=2)
                    last = pe.matmul(dst[:, :, (g % 3) * HG * VW:(g % 3 + 1) * HG * VW], pT[0:nh * SEQ, p % 2, g, :],
                                     vb[0:nh * SEQ, 2 * p:2 * p + 2, o:o + HG, :].rearrange("p i o c -> p i (o c)"),
                                     start=True, stop=True)
                last.then_inc(av_mm, 1)

            def turn_out(p):
                pe.wait_ge(on_ready, p + 1)
                if p == PAIRS - 1:
                    pe.wait_ge(oT_ready, p)
                for k in range(KT):
                    last = pe.transpose(bank[6 + k][:, OT_AT:OT_AT + P], on[:, p % 2, k * P:(k + 1) * P], ident)
                last.then_inc(oT_mm, 1)

            def out_proj(i):
                t0, n = TILES[i]
                if i == 0:
                    pe.wait_ge(mlp_in, 64)
                    pe.wait_ge(dif_ready, PAIRS)
                if i == 3:
                    pe.wait_ge(pT_ready, PAIRS)
                pe.wait_ge(oT_ready, -(-(t0 + n) // (2 * SEQ)))
                for k in range(KT):
                    last = pe.matmul(bank[i][0:n, 0:D], oT[:, k, t0:t0 + n], wo[:, k, :],
                                     start=(k == 0), stop=(k == KT - 1))
                last.then_inc(wo_mm, 1)

            project_v(NT - 1)
            turn_qk(NT - 2)
            scores(0)
            scores(1)
            turn_qk(NT - 1)
            scores(2)
            turn_probs(0)
            for p in range(2, PAIRS):
                if p >= 3:
                    scores(p)
                    turn_out(p - 3)
                turn_probs(p - 1)
                values(p - 2)
            out_proj(0)
            out_proj(1)
            turn_out(PAIRS - 3)
            turn_probs(PAIRS - 1)
            values(PAIRS - 2)
            values(PAIRS - 1)
            out_proj(2)
            turn_out(PAIRS - 2)
            turn_out(PAIRS - 1)
            transpose_tile(1, 0)
            out_proj(3)
            pe.wait_ge(oT_ready, PAIRS)
            transpose_tile(1, 1)
            out_proj(4)
            for s, (h0, h1) in enumerate(PARTS):
                pe.wait_ge(nT_ready[1], -(-h1 // P))
                for j in range(FT):
                    q = s * FT + j
                    if q < 4:
                        pe.wait_ge(x2_ready, q + 1)
                    if FT - 1 - LATE <= q < FT - 1:
                        transpose_tile(1, NT - FT + 1 + q)
                    if q >= 4:
                        pe.wait_ge(hid_ready, q - 3)
                    for k in range(KT):
                        last = pe.matmul(bank[q % 4][:, 0:h1 - h0], w1[:, k, j * P:(j + 1) * P],
                                         nT[:, k, h0:h1], start=(k == 0), stop=(k == KT - 1))
                    last.then_inc(up_mm, 1)
            for i, (t0, n) in enumerate(TILES):
                pe.wait_ge(hid_ready, FT if t0 + n <= PARTS[0][1] else 2 * FT)
                if i == 0:
                    pe.wait_ge(x2_ready, NT)
                if i == 1:
                    pe.wait_ge(nT_ready[1], NT)
                for j in range(FT):
                    last = pe.matmul(bank[(4 + i) % 8][0:n, 0:D], hidT[:, j, t0:t0 + n], w2[:, j, :],
                                     start=(j == 0), stop=(j == FT - 1))
                last.then_inc(down_mm, 1)

            def logits(i):
                t0, n = TILES[i]
                if i == 0:
                    pe.wait_ge(rows_in, 16)
                pe.matmul(bank[3][0:n, i * E:(i + 1) * E], cst("ones")[0:1, 0:n], rows[0:1, 5 * D:],
                          start=True, stop=False)
                pe.wait_ge(nT_ready[2], i + 1)
                for k in range(KT):
                    last = pe.matmul(bank[3][0:n, i * E:(i + 1) * E], nT[:, k, t0:t0 + n], wr[:, k, :],
                                     start=False, stop=(k == KT - 1))
                return last

            transpose_tile(2, 0)
            for i in range(1, NT):
                transpose_tile(2, i)
                logits(i - 1)
            last = logits(NT - 1)
            last.then_inc(logit_mm, 1)
            pe.wait_ge(onehot_ready, 1)
            pe.wait_ge(bf_ready, 2)
            for i in range(NT + 1):
                for j in range(min(i + 1, NT)):
                    last = pe.matmul(bank[4][:, i * E:(i + 1) * E], beforeb[:, :] if j == i else onesb[:, :],
                                     onehotb[:, j, :], start=(j == 0), stop=(j == min(i, NT - 1)))
            last.then_inc(rank_mm, 1)

            def turn_rows(c):
                pe.wait_ge(xe_in, 16 * c)
                for k in range(KT):
                    last = pe.transpose(bank[5][:, k * P:(k + 1) * P], xe[:, k * P:(k + 1) * P], ident)
                last.then_inc(xeT_mm, 1)

            def expert_up(c, first=False):
                if not first:
                    pe.wait_ge(xeT_ready, c + 1)
                for s in range(2):
                    pe.wait_ge(w1s_ready[s], c + 1)
                    if not first:
                        pe.wait_ge(gh_ready[s], c)
                    ahead = first and s == 0
                    order = [(j, k) for k in range(KT) for j in range(4)] if ahead else\
                        [(j, k) for j in range(4) for k in range(KT)]
                    for j, k in order:
                        if ahead and j == 0:
                            pe.wait_ge(xeT_ready if k == KT - 1 else rows0_ready, 1)
                        at = (2 * s + k) * 512 + j * P
                        last = pe.matmul(bank[s][:, j * P:(j + 1) * P], w1s[:, at // D, at % D:at % D + P],
                                         xeT[:, k, :], start=(k == 0 and (j == 0 or not ahead)),
                                         stop=(k == KT - 1), skip_group_check=ahead)
                    last.then_inc(eup_mm[s], 1)

            def expert_down(done, e, dst=bank[6], last_chunk=False, lo=0, hi=FT):
                hidden, ready = (gh, gh_ready) if last_chunk else (eh, eh_ready)
                if lo == 0:
                    pe.wait_ge(ready[0], done)
                    if not last_chunk:
                        pe.wait_ge(y_room, done)
                    pe.matmul(dst[:, 0:D], onesb[0:3, :], ebr[:, ds(e * D, D)], start=True, stop=False)
                for j in range(lo, hi):
                    if j == 4:
                        pe.wait_ge(ready[1], done)
                    last = pe.matmul(dst[:, 0:D], hidden[:, j, :], we[:, ds(e * EXP_W + KT * F + j * D, D)],
                                     start=False, stop=(j == FT - 1))
                if hi == FT:
                    last.then_inc(ey_mm, 1)

            pe.wait_ge(perm_ready, 1)
            pe.wait_ge(shift_ready, 1)
            for k in range(KT):
                for i, (t0, n) in enumerate(TILES):
                    if k == 0 and i == 2:
                        pe.wait_ge(perm_ready, 2)
                    last = pe.matmul(bank[5 + 2 * k][:, 0:P], pay[0:n, i, k * P:(k + 1) * P], perm[0:n, i, :],
                                     start=(i == 0), stop=(i == NT - 1))
                last.then_inc(xeT_mm if k == KT - 1 else rows0_mm, 1)
            n_chunks = chunks_in_use(pe)

            def expert_of(c):
                return pe.value_load(metai[0:1, ds(c, 1)], min_val=0, max_val=E - 1)

            pe.wait_ge(ebr_in, 16)
            for e in range(E):
                pe.wait_ge(we_in[e], 16)
            expert_up(0, first=True)
            e0 = expert_of(0)
            expert_down(1, e0, lo=0, hi=4)
            turn_rows(1)
            expert_down(1, e0, lo=4, hi=6)
            expert_up(1)
            turn_rows(2)
            expert_down(1, e0, lo=6)
            with pe.Fori(2, NCH) as c:
                with pe.If(c < n_chunks):
                    expert_up(c)
                    turn_rows(c + 1)
                    expert_down(c, expert_of(c - 1))
            expert_down(n_chunks, expert_of(n_chunks - 1), bank[7], last_chunk=True)

        @block.vector
        def _(v):
            count = [0]

            def link(ins):
                count[0] += 1
                ins.then_inc(dve, 1)
                v.wait_ge(dve, count[0])

            seen = [0]

            def stats(src, i):
                n = TILES[i][1]
                seen[0] += 1
                link(v.bn_stats(bst[0:n, i, :], src[0:n, i, :]))
                v.bn_aggr(mv[0:n, i, :], bst[0:n, i, :]).then_inc(stat_ready, 1)

            def normalise(l, src, lo, hi, by_pool=0):
                if by_pool:
                    v.wait_ge(root_ready, by_pool)
                else:
                    v.wait_ge(stat_ready, seen[0])
                    vh, y, a, b = (nw[:, j, lo:hi] for j in range(4))
                    inverse_root(v, link, vh, y, a, b, mv[:, lo:hi, 1])
                for i in range(lo, hi):
                    n = TILES[i][1]
                    v.tensor_scalar(nrm[l][0:n, i, 0:D], src[0:n, i, :], mv[0:n, i, 0:1], nw[0:n, 1, i:i + 1],
                                    ALU.subtract, ALU.mult).then_inc(nrm_ready[l], 1)

            def empty_qk(i):
                n = TILES[i][1]
                v.wait_ge(qk_mm, i + 1)
                if i == 0:
                    v.wait_ge(rows_in, 16)
                if i >= 2:
                    v.wait_ge(ropec_ready, i - 1)
                v.tensor_tensor(qk[0:n, i % 2, :], bank[2 * (i % 2)][0:n, :], rows[0:n, 0:2 * D],
                                ALU.add).then_inc(qk_ready, 1)

            def empty_v(i):
                n = TILES[i][1]
                src = bank[6 if i == NT - 1 else 2 * (i % 2) + 1]
                v.wait_ge(v_mm, i + 1)
                v.tensor_tensor(vt[0:n, i, :], src[0:n, 0:D], rows[0:n, 2 * D:3 * D],
                                ALU.add).then_inc(vt_ready, 1)

            def rotate(i):
                n = TILES[i][1]
                v.wait_ge(qk_ready, i + 1)
                if i >= 2:
                    v.wait_ge(rope_ready, i - 1)
                q4 = qk[0:n, i % 2, :].rearrange("p (h a c) -> p h a c", a=2, c=HD // 2)
                s4 = ropes[0:n, i % 2, :].rearrange("p (h a c) -> p h a c", a=2, c=HD // 2)
                sn = cst("sin")[0:n, i * HD:(i + 1) * HD].rearrange("p (o a c) -> p o a c", o=1, a=2)
                for a in range(2):
                    last = v.tensor_tensor(s4[:, :, a, :], q4[:, :, 1 - a, :],
                                           sn[:, :, a, :].broadcast_to((n, 2 * H, HD // 2)), ALU.mult)
                last.then_inc(ropes_ready, 1)

            def mask_keys(i):
                t0, n = TILES[i]
                v.wait_ge(qkT_mm, i + 1)
                src = bank[7][:, 0:n].rearrange("p (o n) -> p o n", o=1).broadcast_to((P, 4, n))
                hm = cst("headmask").rearrange("p (h o) -> p h o", o=1).broadcast_to((P, 4, n))
                v.tensor_tensor(km[:, 0, :, t0:t0 + n], src, hm, ALU.mult).then_inc(km_ready, 1)

            link(v.memset(mv[:, :, :], 1.0))
            link(v.memset(onehotb[:, :, :], 0.0))
            for lo, hi in ((0, 1), (1, 3), (3, NT)):
                for i in range(lo, hi):
                    v.wait_ge(res_ready, i + 1)
                    stats(res, i)
                if lo < 3:
                    normalise(0, res, lo, hi)
            v.wait_ge(const_in, 32)
            for i in range(NT):
                empty_qk(i)
                if i == 0:
                    rotate(i)
                    normalise(0, res, 3, NT, by_pool=1)
                if i < NT - 1:
                    empty_v(i)
                if i > 0:
                    rotate(i)
                if i >= 2:
                    mask_keys(i - 2)
            empty_v(NT - 1)
            mask_keys(NT - 2)

            def soft_in(p):
                v.wait_ge(score_mm, p + 1)
                if p >= 2:
                    v.wait_ge(prob_ready, p - 1)
                s4 = score[p % 2][:, :].rearrange("p (b n) -> p b n", b=2)[:, :, 0:8 * SEQ]\
                    .rearrange("p b (h k) -> p b h k", k=SEQ)
                link(v.tensor_reduce(mx[:, p % 2, :].rearrange("p (b h) -> p b h", b=2), s4, AX, ALU.max))
                v.tensor_tensor(dif[:, p % 2, :].rearrange("p (b h k) -> p b h k", b=2, k=SEQ), s4,
                                mx[:, p % 2, :].rearrange("p (b h o) -> p b h o", b=2, o=1)
                                .broadcast_to((P, 2, 8, SEQ)), ALU.subtract).then_inc(dif_ready, 1)

            def soft_out(p):
                v.wait_ge(av_mm, p + 1)
                if p >= 2:
                    v.wait_ge(oT_mm, p - 1)
                o4 = (bank45 if p == PAIRS - 1 else bank67)[:, :].rearrange("p (b n) -> p b n", b=2)[:, :, 0:2 * HB * VW]\
                    .rearrange("p b (i o c) -> p b i o c", i=2, c=VW)
                for im in range(2):
                    r = slice(64 * im, 64 * im + 64)
                    last = v.reciprocal(rinv[r, p % 2, :].rearrange("p (b h) -> p b h", b=2), o4[r, :, im, :, HD])
                link(last)
                for im in range(2):
                    r = slice(64 * im, 64 * im + 64)
                    last = v.tensor_tensor(
                        on[r, p % 2, :].rearrange("p (b o c) -> p b o c", b=2, c=HD), o4[r, :, im, :, 0:HD],
                        rinv[r, p % 2, :].rearrange("p (b h o) -> p b h o", b=2, o=1)
                        .broadcast_to((64, 2, HB, HD)), ALU.mult)
                last.then_inc(on_ready, 1)

            def add_x2(i):
                n = TILES[i][1]
                v.wait_ge(wo_mm, i + 1)
                v.wait_ge(mid_ready, i + 1)
                v.tensor_tensor(x2[0:n, i, :], bank[i][0:n, 0:D], mid[0:n, i, :], ALU.add).then_inc(x2_ready, 1)
                v.wait_ge(x2_ready, i + 1)
                stats(x2, i)

            soft_in(0)
            mask_keys(NT - 1)
            for p in range(1, PAIRS + 2):
                if p < PAIRS:
                    soft_in(p)
                if p == PAIRS:
                    add_x2(0)
                    add_x2(1)
                if p >= 2:
                    soft_out(p - 2)
            normalise(1, x2, 0, 2, by_pool=2)
            for i in range(2, NT):
                add_x2(i)
            normalise(1, x2, 2, NT)

            v.wait_ge(rows_cleared, 16)
            for lo, hi in ((0, 2), *((i, i + 1) for i in range(2, NT))):
                for i in range(lo, hi):
                    n = TILES[i][1]
                    v.wait_ge(down_mm, i + 1)
                    v.wait_ge(hx_ready, i + 1)
                    link(v.tensor_tensor(mid[0:n, i, :], bank[(4 + i) % 8][0:n, 0:D], res[0:n, i, :], ALU.add))
                    stats(mid, i)
                normalise(2, mid, lo, hi)

            lgb = [P, NT, E]
            v.tensor_copy(pay[:, :, D + 1], cst("tokno")).then_inc(pay_ready, 1)
            v.wait_ge(logit_mm, 1)
            full = NT - 1
            last_n = TILES[full][1]
            lgp = bank[3][:, 0:NT * E].rearrange("p (i e) -> p i e", e=E)
            link(v.tensor_reduce(lmax[:, :], lgp, AX, ALU.max))
            top = lmax[:, :].rearrange("p (i o) -> p i o", o=1).broadcast_to(lgb)
            link(v.tensor_tensor(first[:, :, :], lgp, top, ALU.is_equal))
            v.tensor_tensor(lg[:, :, :], lgp, top, ALU.subtract).then_inc(shift_ready, 1)
            eidx = cst("eidx").rearrange("p (o e) -> p o e", o=1).broadcast_to(lgb)
            link(v.scalar_tensor_tensor(out=first[:, :, :], in0=first[:, :, :], scalar=-float(E), in1=eidx,
                                        op0=ALU.mult, op1=ALU.add))
            link(v.tensor_reduce(row[:, :], first[:, :, :], AX, ALU.min))
            chosen = row[:, :].rearrange("p (i o) -> p i o", o=1).broadcast_to(lgb)
            v.tensor_tensor(onehotb[:, 0:full, :], first[:, 0:full, :], chosen[:, 0:full, :], ALU.is_equal)
            v.tensor_tensor(onehotb[0:last_n, full, :], first[0:last_n, full, :], chosen[0:last_n, full, :],
                            ALU.is_equal).then_inc(onehot_ready, 1)
            link(v.tensor_tensor(onehot[:, :, :], first[:, :, :], chosen, ALU.is_equal))
            v.wait_ge(expl_ready, 1)
            link(v.tensor_reduce(gate[:, :], lg[:, :, :], AX, ALU.add))
            v.reciprocal(pay[:, :, D], gate[:, :]).then_inc(pay_ready, 1)

            v.wait_ge(rank_mm, 1)
            ranks = bank[4][:, 0:NT * E].rearrange("p (i e) -> p i e", e=E)
            t5 = tmp[:, 0:E * NT].rearrange("p (e j) -> p e j", e=E)
            counts = bank[4][:, NT * E:(NT + 1) * E].rearrange("p (e o) -> p e o", o=1)
            link(v.tensor_tensor(t5, counts.broadcast_to((P, E, NT)), cst("thr").rearrange("p (e j) -> p e j", e=E),
                                 ALU.is_gt))
            link(v.tensor_reduce(cnt[:, 1, :], t5, AX, ALU.add))
            t8 = tmp[:, 0:E * E].rearrange("p (a b) -> p a b", a=E)
            link(v.tensor_tensor(t8, cnt[:, 1, :].rearrange("p (o e) -> p o e", o=1).broadcast_to((P, E, E)),
                                 cst("earlier").rearrange("p (a b) -> p a b", a=E), ALU.mult))
            link(v.tensor_reduce(cnt[:, 3, :], t8, AX, ALU.add))
            link(v.scalar_tensor_tensor(out=first[:, :, :],
                                        in0=cnt[:, 3, :].rearrange("p (o e) -> p o e", o=1).broadcast_to(lgb),
                                        scalar=float(CH), in1=ranks, op0=ALU.mult, op1=ALU.add))
            link(v.tensor_tensor(first[:, :, :], first[:, :, :], onehot[:, :, :], ALU.mult))
            link(v.tensor_reduce(row[:, :], first[:, :, :], AX, ALU.add))
            v.tensor_copy(rowi[:, :], row[:, :]).then_inc(row_ready, 1)
            v.wait_ge(logit_mm, 1)
            for lo, hi in ((0, 2), (2, NT)):
                v.tensor_tensor(perm[:, lo:hi, :],
                                row[:, lo:hi].rearrange("p (i o) -> p i o", o=1).broadcast_to((P, hi - lo, CH)),
                                cst("slotno").rearrange("p (o n) -> p o n", o=1).broadcast_to((P, hi - lo, CH)),
                                ALU.is_equal).then_inc(perm_ready, 1)
            link(v.tensor_tensor(cnt[:, 2, :], cnt[:, 3, :], cnt[:, 1, :], ALU.add))
            tc = tmp[:, :].rearrange("p (c e) -> p c e", e=E)
            link(v.tensor_tensor(tc, cnt[:, 2, :].rearrange("p (o e) -> p o e", o=1).broadcast_to((P, NCH + 1, E)),
                                 cst("chunkno").rearrange("p (c e) -> p c e", e=E), ALU.is_le))
            link(v.tensor_reduce(meta[:, :], tc, AX, ALU.add))
            v.tensor_scalar(metai[:, 0:NCH + 1], meta[:, :], float(E - 1), None, ALU.min).then_inc(meta_ready, 1)
            v.tensor_copy(metai[:, NCH + 1:NCH + 2], cnt[:, 2, E - 1:E]).then_inc(meta_ready, 1)

            n_chunks = chunks_in_use(v)

            def keep_rows(c):
                v.wait_ge(xeT_mm, c + 1)
                v.tensor_copy(xeT[:, :, :].rearrange("p k n -> p (k n)"), bank[5][:, 0:2 * P]).then_inc(xeT_ready, 1)
                v.tensor_copy(xk[:, ds(((c + 1) % 4) * ROW_W, ROW_W)], xe).then_inc(xk_ready, 1)

            def keep_hidden(done, before=None):
                for s in range(2):
                    v.wait_ge(gh_ready[s], done)
                    if before is not None and s == 0:
                        v.wait_ge(ey_mm, before)
                    v.tensor_copy(eh[:, 4 * s:4 * s + 4, :], gh[:, 4 * s:4 * s + 4, :]).then_inc(eh_ready[s], 1)

            def step(j, done, ins):
                ins.then_inc(estep[j], 1)
                v.wait_ge(estep[j], done)

            def finish(done, b=0, o=0):
                kept = (done % 4) * ROW_W
                at_step = [0]
                z, st = ez[b], est[:, b, :]

                def link_step(ins):
                    step(at_step[0], done, ins)
                    at_step[0] += 1

                if b == 0:
                    v.wait_ge(eout_ready, 2 * done)
                v.wait_ge(ey_mm, done)
                v.scalar_tensor_tensor(out=z, in0=bank[6 + b][:, 0:D], scalar=xk[:, ds(kept + D, 1)],
                                       in1=xk[:, ds(kept, D)], op0=ALU.mult, op1=ALU.add).then_inc(y_room, 1)
                v.wait_ge(y_room, done + 1)
                link_step(v.bn_stats(st[:, 0:6], z))
                v.tensor_scalar(st[:, 12:13], xk[:, ds(kept + D + 1, 1)], 0.0, 2.0 * TOK, ALU.is_equal, ALU.mult)
                link_step(v.bn_aggr(st[:, 6:8], st[:, 0:6]))
                inverse_root(v, link_step, st[:, 8:9], st[:, 9:10], st[:, 10:11], st[:, 11:12], st[:, 7:8])
                if o == 0:
                    v.wait_ge(eout_room, done)
                v.scalar_tensor_tensor(out=eti[:, o:o + 1], in0=xk[:, ds(kept + D + 1, 1)], scalar=-1.0,
                                       in1=st[:, 12:13], op0=ALU.add, op1=ALU.add).then_inc(eout_ready, 1)
                v.tensor_scalar(eout[o], z, st[:, 6:7], st[:, 9:10], ALU.subtract, ALU.mult).then_inc(eout_ready, 1)

            v.sem_inc(y_room, 1)
            v.sem_inc(eout_room, 1)
            v.sem_inc(eout_ready, 2)
            for k in range(KT):
                v.wait_ge(xeT_mm if k == KT - 1 else rows0_mm, 1)
                v.tensor_copy(xeT[:, k, :], bank[5 + 2 * k][:, 0:P])\
                    .then_inc(xeT_ready if k == KT - 1 else rows0_ready, 1)
            v.sem_inc(xk_ready, 1)
            keep_hidden(1)
            keep_rows(1)
            keep_rows(2)
            v.wait_ge(x0_in, 16)
            with v.Fori(1, NCH) as c:
                with v.If(c < n_chunks):
                    with v.If(c + 1 < n_chunks):
                        keep_hidden(c + 1, before=c)
                        finish(c)
                        keep_rows(c + 2)
                    with v.Else():
                        finish(c, o=2)
                        finish(c + 1, 1, 1)

        @block.scalar
        def _(a):
            def keep_tokens(i):
                n = TILES[i][1]
                a.wait_ge(tok_mm, i + 1)
                a.activation(res[0:n, i, :], bank[i][0:n, 0:D], ACT.Copy).then_inc(res_ready, 1)

            def affine_T(l, i, g, b):
                t0, n = TILES[i]
                a.wait_ge(nT_mm[l], i + 1)
                for k in range(KT):
                    last = a.activation(nT[:, k, t0:t0 + n], bank[5 + i % 2][:, k * P:k * P + n], ACT.Identity,
                                        scale=cols[:, g * KT + k:g * KT + k + 1],
                                        bias=cols[:, b * KT + k:b * KT + k + 1])
                last.then_inc(nT_ready[l], 1)

            def copy_qT(i):
                t0, n = TILES[i]
                a.wait_ge(qkT_mm, i + 1)
                for h in range(4):
                    a.activation(km[:, 1, h, t0:t0 + n], bank[4][:, 2 * P:2 * P + n], ACT.Copy,
                                 scale=cst("headmask")[:, h:h + 1])
                a.activation(qT[:, :, t0:t0 + n], bank[4][:, 0:2 * P].rearrange("p (t n) -> p t n", t=KT)[:, :, 0:n],
                             ACT.Copy).then_inc(qT_ready, 1)

            for i in range(NT - 1):
                keep_tokens(i)
            a.wait_ge(const_in, 32)
            affine_T(0, 0, 0, 1)
            keep_tokens(NT - 1)
            affine_T(0, 1, 0, 1)
            for i in range(NT):
                if i + 2 < NT:
                    affine_T(0, i + 2, 0, 1)
                if i >= 2:
                    copy_qT(i - 2)
            copy_qT(NT - 2)
            copy_qT(NT - 1)

            def exps(p):
                a.wait_ge(dif_ready, p + 1)
                if p >= 2:
                    a.wait_ge(pT_mm, p - 1)
                a.activation(prob[:, p % 2, :], dif[:, p % 2, :], ACT.Exp, scale=float(HD) ** -0.5)\
                    .then_inc(prob_ready, 1)

            def copy_pT(p):
                a.wait_ge(pT_mm, p + 1)
                if p >= 2:
                    a.wait_ge(av_mm, p - 1)
                full = len(GROUPS) - 1
                a.activation(pT[0:HG * SEQ, p % 2, 0:full, :].rearrange("p g n -> p (g n)"),
                             bank45[0:HG * SEQ, 0:full * P], ACT.Copy)
                nh = GROUPS[full][1]
                a.activation(pT[0:nh * SEQ, p % 2, full, :], bank45[0:nh * SEQ, full * P:(full + 1) * P],
                             ACT.Copy).then_inc(pT_ready, 1)

            def copy_oT(p):
                a.wait_ge(oT_mm, p + 1)
                src = bank67[:, :].rearrange("p (t n) -> p t n", t=KT)[:, :, OT_AT:OT_AT + P]\
                    .rearrange("p t (i q) -> p t i q", i=2)[:, :, :, 0:SEQ]
                dst = oT[:, :, 2 * p * SEQ:(2 * p + 2) * SEQ].rearrange("p t (i q) -> p t i q", i=2)
                a.activation(dst, src, ACT.Copy).then_inc(oT_ready, 1)

            for p in range(PAIRS + 3):
                if p >= 3:
                    copy_oT(p - 3)
                if 2 <= p <= PAIRS:
                    copy_pT(p - 1)
                if p < PAIRS:
                    exps(p)
                if p == 1:
                    copy_pT(0)

            for i in range(NT - LATE):
                affine_T(1, i, 2, 3)
            for q in range(2 * FT):
                s, j = divmod(q, FT)
                h0, h1 = PARTS[s]
                if FT - 1 - LATE <= q < FT - 1:
                    affine_T(1, NT - FT + 1 + q, 2, 3)
                a.wait_ge(up_mm, q + 1)
                a.activation(hidT[:, j, h0:h1], bank[q % 4][:, 0:h1 - h0], ACT.Gelu,
                             bias=cols[:, 4 * KT + j:4 * KT + j + 1]).then_inc(hid_ready, 1)
            for i, (t0, n) in enumerate(TILES):
                a.wait_ge(nT_mm[2], i + 1)
                a.activation(nT[:, :, t0:t0 + n],
                             bank[1 + i % 2][:, 0:2 * P].rearrange("p (t n) -> p t n", t=KT)[:, :, 0:n], ACT.Copy)\
                    .then_inc(nT_ready[2], 1)
            a.wait_ge(shift_ready, 1)
            a.activation(lg[:, :, :], lg[:, :, :], ACT.Exp).then_inc(expl_ready, 1)
            a.activation(table[:, :], cst("ones")[:, 0:1], ACT.Gelu)

            n_chunks = chunks_in_use(a)

            def stage(s, e):
                a.activation(w1s[:, 4 * s:4 * s + 4, :].rearrange("p k n -> p (k n)"),
                             we[:, ds(e * EXP_W + s * KT * 512, KT * 512)], ACT.Copy).then_inc(w1s_ready[s], 1)

            def stage_bias(e):
                a.activation(b1s[:, :], b1[:, ds(e * FT, FT)], ACT.Copy).then_inc(b1s_ready, 1)

            def gelu(c, first):
                e = expert_of(c + 1)
                a.wait_ge(b1s_ready, c + 1)
                for s in range(2):
                    a.wait_ge(eup_mm[s], c + 1)
                    if not first:
                        stage(s, e)
                        a.wait_ge(eh_ready[s], c)
                    for j in range(4):
                        last = a.activation(gh[:, 4 * s + j, :], bank[s][:, j * P:(j + 1) * P], ACT.Gelu,
                                            bias=b1s[:, 4 * s + j:4 * s + j + 1])
                    last.then_inc(gh_ready[s], 1)
                    if first:
                        stage(s, e)
                a.wait_ge(gh_ready[1], c + 1)
                stage_bias(e)

            def expert_of(c):
                return a.value_load(metai[0:1, ds(c, 1)], min_val=0, max_val=E - 1)

            a.wait_ge(b1_in, 16)
            for e in range(E):
                a.wait_ge(we_in[e], 16)
            for s in range(2):
                stage(s, expert_of(0))
            stage_bias(expert_of(0))
            gelu(0, True)
            with a.Fori(1, NCH) as c:
                with a.If(c < n_chunks):
                    gelu(c, False)

        @block.gpsimd
        def _(g):
            g.memset(zero, 0.0).then_inc(zero_ready, 1)
            g.wait_ge(const_in, 32)
            g.tensor_copy(beforeb[:, :], cst("before")).then_inc(bf_ready, 1)
            g.tensor_copy(onesb[:, :], cst("ones")).then_inc(bf_ready, 1)
            g.tensor_copy(caus[:, :], cst("causal")).then_inc(mask_ready, 1)
            g.tensor_copy(id64[:, :], cst("id64")).then_inc(mask_ready, 1)
            g.memset(qT[:, :, TOK:QTW], 0.0).then_inc(qpad_ready, 1)
            count = [0]

            def link(ins):
                count[0] += 1
                ins.then_inc(pl, 1)
                g.wait_ge(pl, count[0])

            def roots(lo, hi, stats):
                g.wait_ge(stat_ready, stats)
                vh, y, a, b = (nw[:, j, lo:hi] for j in range(4))
                inverse_root(g, link, vh, y, a, b, mv[:, lo:hi, 1], fused=False)
                g.sem_inc(root_ready, 1)

            roots(3, NT, NT)
            for i, (t0, n) in enumerate(TILES):
                g.wait_ge(qk_ready, i + 1)
                if i >= 2:
                    g.wait_ge(qkT_mm, i - 1)
                cs = cst("cos")[0:n, i * HD:(i + 1) * HD].rearrange("p (o c) -> p o c", o=1).broadcast_to((n, 2 * H, HD))
                g.tensor_tensor(ropec[0:n, i % 2, :].rearrange("p (h c) -> p h c", c=HD),
                                qk[0:n, i % 2, :].rearrange("p (h c) -> p h c", c=HD), cs, ALU.mult)\
                    .then_inc(ropec_ready, 1)
                g.wait_ge(ropec_ready, i + 1)
                g.wait_ge(ropes_ready, i + 1)
                g.tensor_tensor(ropec[0:n, i % 2, :], ropec[0:n, i % 2, :], ropes[0:n, i % 2, :],
                                ALU.add).then_inc(rope_ready, 1)
            R = HG * SEQ
            vm = cst("vmask")[0:R, :].rearrange("p (i o c) -> p i o c", i=1, c=VW)
            g.tensor_copy(vb[0:R, :, 0:H, HD], vm[:, :, :, HD].broadcast_to((R, IMGS, H)))
            g.memset(vb[0:R, :, H:HO, 0:HD], 0.0)
            g.memset(vb[0:R, :, H:HO, HD], 1.0).then_inc(vb_ready, 1)
            for p in range(PAIRS):
                if p == 0:
                    g.wait_ge(vrep_in[0], 16 * HG)
                if 2 * p == EARLY_IMGS:
                    g.wait_ge(vrep_in[1], 16 * HG)
                src = vrep[0:R, 2 * p:2 * p + 2, :].rearrange("p i (o c) -> p i o c", c=HD)
                g.tensor_tensor(vb[0:R, 2 * p:2 * p + 2, 0:H, 0:HD], src, vm[:, :, :, 0:HD].broadcast_to((R, 2, H, HD)), ALU.mult)\
                    .then_inc(vb_ready, 1)
            g.wait_ge(eb_in, 16)
            for s in range(3):
                g.tensor_copy(ebp[:, s, :], ebf[:, s, :]).then_inc(eb_split, 1)
                g.wait_ge(eb_split, s + 1)
                if s < 2:
                    g.tensor_tensor(ebf[:, s + 1, :], ebf[:, s, :], ebp[:, s, :], ALU.subtract).then_inc(eb_rest, 1)
                    g.wait_ge(eb_rest, s + 1)
            for i, (t0, n) in enumerate(TILES):
                g.wait_ge(res_ready, i + 1)
                g.tensor_tensor(mid[0:n, i, :], res[0:n, i, :], rows[0:n, 3 * D:4 * D], ALU.add).then_inc(mid_ready, 1)
            roots(0, 2, NT + 2)
            for i, (t0, n) in enumerate(TILES):
                g.wait_ge(x2_ready, i + 1)
                link(g.tensor_tensor(res[0:n, i, :], res[0:n, i, :], x2[0:n, i, :], ALU.add))
                g.tensor_tensor(res[0:n, i, :], res[0:n, i, :], rows[0:n, 4 * D:5 * D], ALU.add).then_inc(hx_ready, 1)
            g.wait_ge(row_ready, 1)
            g.wait_ge(pay_ready, 2)
            g.wait_ge(rows_cleared, 16)
            for i, (t0, n) in enumerate(TILES):
                g.indirect_dma_start(xs_dram, bass.IndirectOffsetOnAxis(rowi[0:n, i:i + 1], 0), pay[0:n, i, :], None)\
                    .then_inc(xs_out, 16)
            n_chunks = chunks_in_use(g)

            def store(done, o=0):
                g.wait_ge(eout_ready, 2 * done + 2)
                g.sem_inc(store_begun, 1)
                g.indirect_dma_start(out_d, bass.IndirectOffsetOnAxis(eti[:, o:o + 1], 0), eout[o], None,
                                     bounds_check=TOK - 1, oob_is_err=False).then_inc(out_st, 16)
                if o == 0:
                    g.wait_ge(out_st, 16 * done)
                    g.sem_inc(eout_room, 1)

            store(1)
            with g.Fori(2, NCH) as c:
                with g.If(c < n_chunks):
                    with g.If(c + 1 < n_chunks):
                        store(c)
                    with g.Else():
                        store(c, 2)
                        store(c + 1, 1)
            g.wait_ge(out_st, 16 * n_chunks)


def kernel(x, L0_tok_W, L0_attn_ln1_g, L0_attn_ln1_b, L0_attn_Wqkv, L0_attn_bqkv, L0_attn_Wo, L0_attn_bo,
           L0_attn_ln2_g, L0_attn_ln2_b, L0_attn_W1, L0_attn_b1, L0_attn_W2, L0_attn_b2, L0_ffn_W1, L0_ffn_b1,
           L0_ffn_W2, L0_ffn_b2, L0_ffn_Wr, L0_ffn_br):
    import concourse.bacc as bacc
    from concourse.bass_utils import run_bass_kernel_spmd

    def on_partitions(w):
        w = np.asarray(w)
        return w.reshape(-1, P, w.shape[-1]).transpose(1, 0, 2)

    heads = [t * 8 + half * 4 + h4 for half in range(2) for t in range(2) for h4 in range(4)]
    slot_cols = np.concatenate([np.arange(h * HD, (h + 1) * HD) for h in heads])
    qkv_cols = np.concatenate([np.arange(2 * D), 2 * D + slot_cols])

    patches = np.asarray(x).reshape(IMGS, 3, 6, 16, 6, 16).transpose(0, 1, 3, 5, 2, 4).reshape(TOK, 3 * 256).T
    w1e, w2e = np.asarray(L0_ffn_W1), np.asarray(L0_ffn_W2)
    experts = np.concatenate([w1e.reshape(E, KT, P, 2, F // 2).transpose(0, 2, 3, 1, 4).reshape(E, P, KT * F),
                              w2e.reshape(E, FT, P, D).transpose(0, 2, 1, 3).reshape(E, P, FT * D)], axis=2)
    rows = np.concatenate([np.asarray(L0_attn_bqkv)[qkv_cols], np.asarray(L0_attn_bo), np.asarray(L0_attn_b2),
                           np.asarray(L0_ffn_br)])[None, :]
    cols = np.concatenate([np.asarray(a).reshape(-1, P).T for a in
                           (L0_attn_ln1_g, L0_attn_ln1_b, L0_attn_ln2_g, L0_attn_ln2_b, L0_attn_b1)], axis=1)
    arrays = {
        "xT": on_partitions(patches), "tokw": on_partitions(L0_tok_W),
        "wqkv": on_partitions(np.asarray(L0_attn_Wqkv)[:, qkv_cols]),
        "wo": on_partitions(np.asarray(L0_attn_Wo)[slot_cols]), "w1": on_partitions(L0_attn_W1),
        "w2": on_partitions(L0_attn_W2), "we": experts, "wr": on_partitions(L0_ffn_Wr),
        "b1": np.asarray(L0_ffn_b1).reshape(E * FT, P).T, "rows": rows, "cols": cols,
        "eb": np.asarray(L0_ffn_b2).reshape(P, -1), "consts": shape_constants(),
    }
    nc = bacc.Bacc("TRN2", target_bir_lowering=False, num_devices=1)
    arrays = {k: np.ascontiguousarray(a) for k, a in arrays.items()}
    args = [nc.dram_tensor(k + "_in", a.shape, F32, kind="ExternalInput").ap() for k, a in arrays.items()]
    out = nc.dram_tensor("out", (TOK, D), F32, kind="ExternalOutput").ap()
    tower(nc, *args, out)
    r = run_bass_kernel_spmd(nc, [{k + "_in": a for k, a in arrays.items()}], core_ids=[0])
    return r.results[0]["out"].reshape(IMGS, SEQ, D)
```
